# Optimizing a Trainium2 kernel written in Bass

```python
import numpy as np
import jax
import jax.numpy as jnp

def _softmax(x, axis=-1):
    return jax.nn.softmax(x, axis=axis)

def _gelu(x):
    return jax.nn.gelu(x, approximate=True)

def _silu(x):
    return jax.nn.silu(x)

def _sigmoid(x):
    return jax.nn.sigmoid(x)

def _layernorm(x, axis=-1, eps=1e-05):
    m = jnp.mean(x, axis=axis, keepdims=True)
    v = jnp.var(x, axis=axis, keepdims=True)
    return (x - m) / jnp.sqrt(v + eps)

def _scatter_add(tgt, idx, src, axis=0):
    return tgt.at[idx].add(src)

def _segment_sum(src, seg, n):
    return jax.ops.segment_sum(src, seg, n)
kernel_name = 'mk_prb_d2_jaxref_r4_85ad11'

def setup_inputs(seed: int=0):
    np.random.seed(seed)
    _w = jnp.asarray

    def _L0_attn_setup():
        import jax, jax.numpy as jnp
        import numpy as np
        import math
        B, N, D, H = (1, 1024, 256, 16)
        HS = D // H
        NEG_INF = -10000.0
        key = jax.random.key(seed)
        k1, k2, k3, k4, k5 = jax.random.split(key, 5)
        return {'encodings': jax.random.normal(k1, (B, N, D), dtype=jnp.float32), 'attn_W': jax.random.normal(k2, (D, 3 * D), dtype=jnp.float32) * 0.02, 'attn_b': jax.random.normal(k3, (3 * D,), dtype=jnp.float32) * 0.02, 'out_W': jax.random.normal(k4, (D, D), dtype=jnp.float32) * 0.02, 'out_b': jax.random.normal(k5, (D,), dtype=jnp.float32) * 0.02}
    _L0_attn_in = _L0_attn_setup()

    def _L0_ffn_setup():
        import jax, jax.numpy as jnp
        import numpy as np
        B, S, H, E = (4, 512, 256, 8)
        key = jax.random.key(seed)
        k1, k2, k3 = jax.random.split(key, 3)
        scale_w = 1.0 / np.sqrt(H)
        return {'x': jax.random.normal(k1, (B, S, H), dtype=jnp.float32), 'router_w': jax.random.normal(k2, (H, E), dtype=jnp.float32) * scale_w, 'router_b': jnp.zeros((E,), dtype=jnp.float32), 'expert_w': jax.random.normal(k3, (E, H, H), dtype=jnp.float32) * scale_w, 'expert_b': jnp.zeros((E, H), dtype=jnp.float32)}
    _L0_ffn_in = _L0_ffn_setup()

    def _L1_attn_setup():
        import jax, jax.numpy as jnp
        import numpy as np
        EPS = 1e-06
        N_HEADS = 16

        def _project_static(x):
            sp = jnp.clip(x[..., 1:], -8.0, 8.0)
            x0 = jnp.sqrt(1.0 + jnp.sum(sp * sp, axis=-1, keepdims=True) + EPS)
            return jnp.concatenate([x0, sp], axis=-1)

        def _inner_static(x, y):
            return -x[..., 0] * y[..., 0] + jnp.sum(x[..., 1:] * y[..., 1:], axis=-1)

        def _log_map_approx(x, y):
            y = _project_static(y)
            xy = _inner_static(x, y)
            xy = jnp.minimum(xy, -(1.0 + EPS))[..., None]
            d = jnp.maximum(jnp.arccosh(jnp.maximum(-xy, 1.0 + EPS)), 0.001)
            dirv = y + xy * x
            dn = jnp.sqrt(jnp.maximum(_inner_static(dirv, dirv), EPS))[..., None]
            return d * dirv / (dn + EPS)

        def _dynamic_metric(x, mu, W1, b1, W2, b2):
            d = x.shape[-1]
            eta = jnp.ones((d,), x.dtype).at[0].set(-1.0)
            v = x - mu
            h = jnp.tanh(jnp.tanh(v @ W1.T + b1) @ W2.T + b2) * 0.1
            g = eta + h
            return jnp.concatenate([-jnp.abs(g[..., :1]), jnp.abs(g[..., 1:])], axis=-1)
        key = jax.random.key(seed)
        ks = jax.random.split(key, 9)
        B, T, d = (2, 512, 256)
        s = 0.02
        return {'x': jax.random.normal(ks[0], (B, T, d), jnp.float32), 'W1': jax.random.normal(ks[1], (2 * d, d), jnp.float32) * s, 'b1': jax.random.normal(ks[2], (2 * d,), jnp.float32) * s, 'W2': jax.random.normal(ks[3], (d, 2 * d), jnp.float32) * s, 'b2': jax.random.normal(ks[4], (d,), jnp.float32) * s, 'Wq': jax.random.normal(ks[5], (d, d), jnp.float32) * s, 'Wk': jax.random.normal(ks[6], (d, d), jnp.float32) * s, 'Wv': jax.random.normal(ks[7], (d, d), jnp.float32) * s, 'Wo': jax.random.normal(ks[8], (d, d), jnp.float32) * s}
    _L1_attn_in = _L1_attn_setup()

    def _L1_ffn_setup():
        import jax, jax.numpy as jnp
        import numpy as np
        D_MODEL = 256
        EXPANSION = 4
        D_HIDDEN = D_MODEL * EXPANSION
        NUM_STAGES = int(np.log2(D_HIDDEN))

        def butterfly(y, weights, dim):
            lead = y.shape[:-1]
            for stage in range(weights.shape[0]):
                s = 2 ** stage
                nb = dim // (2 * s)
                yr = y.reshape(*lead, nb, 2, s)
                a = yr[..., 0, :]
                b = yr[..., 1, :]
                w = weights[stage].reshape(nb, s, 2, 2)
                na = w[..., 0, 0] * a + w[..., 0, 1] * b
                nb2 = w[..., 1, 0] * a + w[..., 1, 1] * b
                y = jnp.stack([na, nb2], axis=-2).reshape(*lead, dim)
            return y
        key = jax.random.key(seed)
        ks = jax.random.split(key, 6)
        B, S = (4, 512)
        x = jax.random.normal(ks[0], (B, S, D_MODEL), jnp.float32)
        W_exp = jax.random.normal(ks[1], (D_MODEL, D_HIDDEN), jnp.float32) * 0.02
        b_exp = jnp.zeros((D_HIDDEN,), jnp.float32)
        up_weights = jax.random.normal(ks[2], (NUM_STAGES, D_HIDDEN // 2, 2, 2), jnp.float32) * 0.02
        up_bias = jnp.zeros((D_HIDDEN,), jnp.float32)
        down_weights = jax.random.normal(ks[3], (NUM_STAGES, D_HIDDEN // 2, 2, 2), jnp.float32) * 0.02
        W_con = jax.random.normal(ks[4], (D_HIDDEN, D_MODEL), jnp.float32) * 0.02
        b_con = jnp.zeros((D_MODEL,), jnp.float32)
        down_bias = jnp.zeros((D_MODEL,), jnp.float32)
        return dict(x=x, W_exp=W_exp, b_exp=b_exp, up_weights=up_weights, up_bias=up_bias, down_weights=down_weights, W_con=W_con, b_con=b_con, down_bias=down_bias)
    _L1_ffn_in = _L1_ffn_setup()
    _d = {'L0_attn_encodings': _L0_attn_in['encodings'], 'L0_attn_attn_W': _L0_attn_in['attn_W'], 'L0_attn_attn_b': _L0_attn_in['attn_b'], 'L0_attn_out_W': _L0_attn_in['out_W'], 'L0_attn_out_b': _L0_attn_in['out_b'], 'L0_ffn_router_w': _L0_ffn_in['router_w'], 'L0_ffn_router_b': _L0_ffn_in['router_b'], 'L0_ffn_expert_w': _L0_ffn_in['expert_w'], 'L0_ffn_expert_b': _L0_ffn_in['expert_b'], 'L1_attn_W1': _L1_attn_in['W1'], 'L1_attn_b1': _L1_attn_in['b1'], 'L1_attn_W2': _L1_attn_in['W2'], 'L1_attn_b2': _L1_attn_in['b2'], 'L1_attn_Wq': _L1_attn_in['Wq'], 'L1_attn_Wk': _L1_attn_in['Wk'], 'L1_attn_Wv': _L1_attn_in['Wv'], 'L1_attn_Wo': _L1_attn_in['Wo'], 'L1_ffn_W_exp': _L1_ffn_in['W_exp'], 'L1_ffn_b_exp': _L1_ffn_in['b_exp'], 'L1_ffn_up_weights': _L1_ffn_in['up_weights'], 'L1_ffn_up_bias': _L1_ffn_in['up_bias'], 'L1_ffn_down_weights': _L1_ffn_in['down_weights'], 'L1_ffn_W_con': _L1_ffn_in['W_con'], 'L1_ffn_b_con': _L1_ffn_in['b_con'], 'L1_ffn_down_bias': _L1_ffn_in['down_bias']}
    _x0 = _d['L0_attn_encodings']
    _d['L0_attn_encodings'] = jax.random.normal(jax.random.fold_in(jax.random.key(seed), 1), (8, 1024, 256), dtype=_x0.dtype)
    del _x0
    return _d

def reference(L0_attn_encodings, L0_attn_attn_W, L0_attn_attn_b, L0_attn_out_W, L0_attn_out_b, L0_ffn_router_w, L0_ffn_router_b, L0_ffn_expert_w, L0_ffn_expert_b, L1_attn_W1, L1_attn_b1, L1_attn_W2, L1_attn_b2, L1_attn_Wq, L1_attn_Wk, L1_attn_Wv, L1_attn_Wo, L1_ffn_W_exp, L1_ffn_b_exp, L1_ffn_up_weights, L1_ffn_up_bias, L1_ffn_down_weights, L1_ffn_W_con, L1_ffn_b_con, L1_ffn_down_bias):

    def _L0_attn_ref(encodings, attn_W, attn_b, out_W, out_b):
        import jax, jax.numpy as jnp
        import numpy as np
        import math
        B, N, D, H = (1, 1024, 256, 16)
        HS = D // H
        NEG_INF = -10000.0
        b, n, d = encodings.shape
        qkv = encodings @ attn_W + attn_b
        qkv = qkv.reshape(b, n, H, 3 * HS).transpose(0, 2, 1, 3)
        q, k, v = jnp.split(qkv, 3, axis=-1)
        scores = jnp.einsum('bhki,bhqi->bhkq', k, q) / math.sqrt(HS)
        mask = jnp.arange(n)[:, None] <= jnp.arange(n)[None, :]
        scores = jnp.where(mask, scores, jnp.float32(NEG_INF))
        prob = jax.nn.softmax(scores, axis=2)
        combined = jnp.einsum('bhkq,bhkl->bhql', prob, v)
        out = combined.transpose(0, 2, 1, 3).reshape(b, n, d)
        return out @ out_W + out_b

    def _L0_ffn_ref(x, router_w, router_b, expert_w, expert_b):
        import jax, jax.numpy as jnp
        import numpy as np
        B, S, H, E = (4, 512, 256, 8)
        b, s, h = x.shape
        xt = x.reshape(b * s, h)
        logits = xt @ router_w + router_b
        probs = jax.nn.softmax(logits, axis=-1)
        gate = jnp.max(probs, axis=-1)
        idx = jnp.argmax(probs, axis=-1)
        out_all = jnp.einsum('th,ehd->ted', xt, expert_w) + expert_b[None, :, :]
        e_out = jnp.take_along_axis(out_all, idx[:, None, None], axis=1)[:, 0, :]
        y = gate[:, None] * e_out
        return y.reshape(b, s, h)

    def _L1_attn_ref(x, W1, b1, W2, b2, Wq, Wk, Wv, Wo):
        import jax, jax.numpy as jnp
        import numpy as np
        EPS = 1e-06
        N_HEADS = 16

        def _project_static(x):
            sp = jnp.clip(x[..., 1:], -8.0, 8.0)
            x0 = jnp.sqrt(1.0 + jnp.sum(sp * sp, axis=-1, keepdims=True) + EPS)
            return jnp.concatenate([x0, sp], axis=-1)

        def _inner_static(x, y):
            return -x[..., 0] * y[..., 0] + jnp.sum(x[..., 1:] * y[..., 1:], axis=-1)

        def _log_map_approx(x, y):
            y = _project_static(y)
            xy = _inner_static(x, y)
            xy = jnp.minimum(xy, -(1.0 + EPS))[..., None]
            d = jnp.maximum(jnp.arccosh(jnp.maximum(-xy, 1.0 + EPS)), 0.001)
            dirv = y + xy * x
            dn = jnp.sqrt(jnp.maximum(_inner_static(dirv, dirv), EPS))[..., None]
            return d * dirv / (dn + EPS)

        def _dynamic_metric(x, mu, W1, b1, W2, b2):
            d = x.shape[-1]
            eta = jnp.ones((d,), x.dtype).at[0].set(-1.0)
            v = x - mu
            h = jnp.tanh(jnp.tanh(v @ W1.T + b1) @ W2.T + b2) * 0.1
            g = eta + h
            return jnp.concatenate([-jnp.abs(g[..., :1]), jnp.abs(g[..., 1:])], axis=-1)
        B, T, d = x.shape
        h, dh = (N_HEADS, d // N_HEADS)
        mu = jnp.zeros((d,), x.dtype).at[0].set(1.0)
        mu = jnp.broadcast_to(mu, (B, T, d))
        v = _log_map_approx(mu, x)
        q = (v @ Wq.T).reshape(B, T, h, dh).transpose(0, 2, 1, 3)
        k = (v @ Wk.T).reshape(B, T, h, dh).transpose(0, 2, 1, 3)
        vv = (v @ Wv.T).reshape(B, T, h, dh).transpose(0, 2, 1, 3)
        g_x = _dynamic_metric(x, mu, W1, b1, W2, b2)
        gh = g_x.reshape(B, T, h, dh).transpose(0, 2, 1, 3)
        sc = jnp.einsum('bhqd,bhkd->bhqk', q * gh, k) / jnp.sqrt(jnp.asarray(dh, x.dtype))
        at = jax.nn.softmax(sc, axis=-1)
        out = jnp.einsum('bhqk,bhkd->bhqd', at, vv).transpose(0, 2, 1, 3).reshape(B, T, d)
        out = out @ Wo.T
        return _project_static(_project_static(mu) + out * 0.1)

    def _L1_ffn_ref(x, W_exp, b_exp, up_weights, up_bias, down_weights, W_con, b_con, down_bias):
        import jax, jax.numpy as jnp
        import numpy as np
        D_MODEL = 256
        EXPANSION = 4
        D_HIDDEN = D_MODEL * EXPANSION
        NUM_STAGES = int(np.log2(D_HIDDEN))

        def butterfly(y, weights, dim):
            lead = y.shape[:-1]
            for stage in range(weights.shape[0]):
                s = 2 ** stage
                nb = dim // (2 * s)
                yr = y.reshape(*lead, nb, 2, s)
                a = yr[..., 0, :]
                b = yr[..., 1, :]
                w = weights[stage].reshape(nb, s, 2, 2)
                na = w[..., 0, 0] * a + w[..., 0, 1] * b
                nb2 = w[..., 1, 0] * a + w[..., 1, 1] * b
                y = jnp.stack([na, nb2], axis=-2).reshape(*lead, dim)
            return y
        h = jnp.einsum('bsd,dh->bsh', x, W_exp) + b_exp
        h = butterfly(h, up_weights, D_HIDDEN)
        h = jax.nn.gelu(h + up_bias, approximate=False)
        h = butterfly(h, down_weights, D_HIDDEN)
        y = jnp.einsum('bsh,hd->bsd', h, W_con) + b_con
        return y + down_bias
    x = L0_attn_encodings
    xn = _layernorm(x, axis=-1)
    x = x + _L0_attn_ref(xn, L0_attn_attn_W, L0_attn_attn_b, L0_attn_out_W, L0_attn_out_b) + _L0_ffn_ref(xn, L0_ffn_router_w, L0_ffn_router_b, L0_ffn_expert_w, L0_ffn_expert_b)
    xn = _layernorm(x, axis=-1)
    x = x + _L1_attn_ref(xn, L1_attn_W1, L1_attn_b1, L1_attn_W2, L1_attn_b2, L1_attn_Wq, L1_attn_Wk, L1_attn_Wv, L1_attn_Wo) + _L1_ffn_ref(xn, L1_ffn_W_exp, L1_ffn_b_exp, L1_ffn_up_weights, L1_ffn_up_bias, L1_ffn_down_weights, L1_ffn_W_con, L1_ffn_b_con, L1_ffn_down_bias)
    return x

_drawn_inputs = setup_inputs


def setup_inputs(seed=0):
    import zlib

    import numpy as np

    out = dict(_drawn_inputs(seed))
    spreads = {'L0_ffn_router_b': (0.0, 0.1),
     'L0_ffn_expert_b': (0.0, 0.548),
     'L1_ffn_b_exp': (0.0, 0.1),
     'L1_ffn_up_bias': (0.0, 0.1),
     'L1_ffn_b_con': (0.0, 0.652),
     'L1_ffn_down_bias': (0.0, 0.667)}
    factors = {'L0_attn_attn_W': 6.815,
     'L0_attn_attn_b': 8.0,
     'L0_attn_out_W': 5.501,
     'L0_attn_out_b': 3.161,
     'L1_attn_W1': 64.0,
     'L1_attn_b1': 64.0,
     'L1_attn_W2': 64.0,
     'L1_attn_b2': 64.0,
     'L1_attn_Wq': 64.0,
     'L1_attn_Wk': 64.0,
     'L1_attn_Wv': 56.909,
     'L1_attn_Wo': 56.172}
    for name, (base, spread) in spreads.items():
        noise = np.random.default_rng([zlib.crc32(name.encode()), seed]).standard_normal(out[name].shape)
        drawn = base * np.exp(spread * noise) if base else spread * noise
        out[name] = jnp.asarray(drawn.astype(out[name].dtype))
    for name, factor in factors.items():
        out[name] = (out[name] * factor).astype(out[name].dtype)
    return out
```

```python
from contextlib import ExitStack

import numpy as np

import concourse.bass as bass
from concourse import mybir

F32 = mybir.dt.float32
BF16 = mybir.dt.bfloat16
ALU = mybir.AluOpType
ACT = mybir.ActivationFunctionType
AX = mybir.AxisListType.X

P = 128
NB, T, D = 8, 1024, 256
H, HS = 16, 16
QH = 4
NQ = H // QH
TT = T // P
KC = D // P
NE = 8
FH = 1024
HT = FH // P
MH = 2 * D
MT = MH // P
STAGES = 10
HALF = 512
BLK = HS
Q_ORDER = (0, 0, 1, 0, 2, 1)
K_ORDER = (0, 1, 0, 2, 0, 1)
SROWS = BLK * len(Q_ORDER)
MROWS = 3
SCALE = HS ** -0.5
NEG = -1.0e30
BIG = 3.0e38
VC = HS + 1
LN_EPS = 1e-5
EPS = 1e-6


class Counter:

    def __init__(self, sem):
        self.sem, self.n = sem, 0

    def add(self, by):
        self.n += by
        return self, self.n


class Lane:

    def __init__(self, name, counter):
        self.name, self.counter, self.queue, self.known = name, counter, [], {}

    def wait(self, *marks):
        for m in marks:
            if m is None:
                continue
            counter, value = m
            if self.known.get(id(counter), 0) < value:
                self.known[id(counter)] = value
                self.queue.append(lambda eng, s=counter.sem, v=value: eng.wait_ge(s, v))

    def do(self, fn, *marks, done=None, by=1, signal=True):
        self.wait(*marks)
        if not signal:
            self.queue.append(lambda eng: fn(eng))
            return None
        counter = done or self.counter
        mark = counter.add(by)
        self.queue.append(lambda eng, s=counter.sem: fn(eng).then_inc(s, by))
        return mark

    def run(self, eng):
        for step in self.queue:
            step(eng)


def two_layers(nc, ctx, a, out):
    def sb(name, shape, dt=F32):
        return ctx.enter_context(nc.sbuf_tensor(name, shape, dt))

    def bank(name):
        return ctx.enter_context(nc.psum_tensor(name, [P, HALF], F32))

    def sem(name):
        return Counter(ctx.enter_context(nc.semaphore(name)))

    pe = Lane("pe", sem("pe_done"))
    act = Lane("act", sem("act_done"))
    dve = Lane("dve", sem("dve_done"))
    pool = Lane("pool", sem("pool_done"))
    sp = Lane("sp", None)
    pe_scores, pe_max = sem("pe_scores"), sem("pe_max")
    act_exp, dve_max = sem("act_exp"), sem("dve_max")
    weights_in = sem("weights_in")

    def load(dst, src, counter, *marks):
        return sp.do(lambda e: e.dma_start(dst, src), *marks, done=counter, by=16)

    max_bank = [bank("max0"), bank("max1")]
    score_bank = [bank("score0"), bank("score1")]
    pv_bank = [bank("pv0"), bank("pv1")]
    chain_bank, bulk_bank = bank("chain"), bank("bulk")
    max_free, score_free, pv_free = [None, None], [None, None], [None, None]
    free = {"chain": None, "bulk": None}

    ident, ident_bf = sb("ident", [P, P]), sb("ident_bf", [P, P], BF16)
    causal = sb("causal", [P, P], BF16)
    ones_row = sb("ones_row", [1, P])
    power = sb("power", [P, 2, TT])
    w0qk, b0qk = sb("w0qk", [P, KC, NQ, P]), sb("b0qk", [P, NQ])
    w0v, b0v = sb("w0v", [P, KC, D]), sb("b0v", [P, D])
    w0o, b0o = sb("w0o", [P, KC, D]), sb("b0o", [1, D])
    rw, rb = sb("rw", [P, KC, NE]), sb("rb", [P, NE])
    expert_b = sb("expert_b", [NE, D])
    first_wins = sb("first_wins", [P, TT, NE])
    w1qk, w1v, w1o = sb("w1qk", [P, KC, NQ, P]), sb("w1v", [P, KC, D]), sb("w1o", [P, KC, D])
    wm1, bm1, wm1c = sb("wm1", [P, KC, MH]), sb("bm1", [P, MT]), sb("wm1c", [P, MT])
    wm2, bm2, eta = sb("wm2", [P, MT, 2, P]), sb("bm2", [P, 2]), sb("eta", [P, 2])
    wexp, bexp = sb("wexp", [P, KC, FH]), sb("bexp", [P, HT])
    upb = sb("upb", [P, HT])
    wcon = sb("wcon", [P, HT, D])
    bcon = sb("bcon", [1, D])
    w_expert = [sb(f"w_expert{i}", [P, KC, D]) for i in range(2)]

    qstack = [sb(f"qstack{i}", [P, QH, T], BF16) for i in range(3)]
    kstack = [sb(f"kstack{i}", [P, QH, T], BF16) for i in range(3)]
    values = [sb(f"values{i}", [P, TT, H, VC]) for i in range(2)]
    prob = [sb(f"prob{i}", [P, QH, HALF]) for i in range(2)]
    srcT = [sb(f"srcT{i}", [P, KC, T]) for i in range(2)]
    normT = sb("normT", [P, KC, T])
    acc = [sb(f"acc{i}", [P, TT, D]) for i in range(2)]
    tok = [sb(f"tok{i}", [P, TT, D]) for i in range(2)]
    part = [sb(f"part{i}", [P, T], BF16) for i in range(3)]
    rest, gated = sb("rest", [P, HALF]), sb("gated", [P, HALF])
    hid = sb("hid", [P, 4 * HALF])
    metric = sb("metric", [P, 2, T])
    turned = sb("turned", [P, HALF])
    maxes = [sb(f"maxes{i}", [P, 2, QH, TT]) for i in range(2)]
    negmax = sb("negmax", [P, QH * TT])
    mrest = sb("mrest", [QH * TT, P])
    mpart = [sb("mpart", [QH * TT, 3, P], BF16)] * 2
    stats, mv = sb("stats", [P, TT, 6]), sb("mv", [P, TT, 2])
    small = sb("small", [P, 12, TT])
    rstd = sb("rstd", [P, TT])
    recip = sb("recip", [P, 4, QH])
    logit = sb("logit", [P, TT, NE])
    lwork = sb("lwork", [P, TT, NE])
    lmax, lsum = sb("lmax", [P, TT]), sb("lsum", [P, TT])
    gate_w = [sb(f"gate_w{i}", [P, TT, NE]) for i in range(2)]
    gateT = sb("gateT", [NE, T])
    x1_dram = nc.dram_tensor("x1_scratch", [NB, P, TT, D], F32, kind="Internal").ap()
    bf_w = metric[:, :, :].rearrange("p a b -> p (a b)").rearrange("p (c j) -> p c j", c=4)
    bf_t = hid[:, :].rearrange("p (c j) -> p c j", c=4)
    bias_row, dbias = normT[0:1, 0, :], normT[0:1, 1, 0:D]

    def bcast(ap, n, p=P):
        return ap.rearrange("(o n) -> o n", o=1).to_broadcast((p, n))

    W = {}

    def weight(name, dst, src):
        W[name] = load(dst, src, weights_in)

    x_in = [sem("x_in0"), sem("x_in1")]
    acc_out = [sem("acc_out0"), sem("acc_out1")]
    x_dram = a["x"].rearrange("b (t p) d -> b p t d", p=P, t=TT)
    out_dram = out.rearrange("b (t p) d -> b p t d", p=P, t=TT)
    acc_loaded = {}
    acc_loaded[0] = load(acc[0][:], x_dram[0], x_in[0])
    weight("qk0", w0qk[:], a["w0qk"])
    weight("v0", w0v[:], a["w0v"])
    weight("rw", rw[:], a["rw"])
    weight("b0qk", b0qk[:], a["b0qk"])
    weight("b0v", b0v[:], bcast(a["b0v"], D))
    weight("rb", rb[:], bcast(a["rb"], NE))
    weight("o0", w0o[:], a["w0o"])
    weight("b0o", b0o[:], a["b0o"])
    weight("eb", expert_b[:], a["expert_b"])
    weight("wexp", wexp[:], a["wexp"])
    weight("bexp", bias_row, a["b_exp"])
    weight("upb", upb[:], a["upb"])
    weight("bcon", bcon[:], a["b_con"])
    weight("dbias", dbias, a["down_bias"])
    weight("qk1", w1qk[:], a["w1qk"])
    weight("v1", w1v[:], a["w1v"])
    weight("o1", w1o[:], a["w1o"])
    weight("m1", wm1[:], a["wm1"])
    weight("bm1", bm1[:], a["bm1"])
    weight("m1c", wm1c[:], a["wm1c"])
    weight("m2", wm2[:], a["wm2"])
    weight("bm2", bm2[:], a["bm2"])
    all_weights = (weights_in, weights_in.n)

    zeroed = pool.do(lambda e: e.memset(ident[:], 0.0))
    id_ready = pool.do(lambda e: e.affine_select(out=ident[:], in_=ident[:], compare_op=ALU.not_equal,
                                                 fill=1.0, base=0, pattern=[[-1, P]],
                                                 channel_multiplier=1), zeroed)
    zeroed = pool.do(lambda e: e.memset(ident_bf[:], 0.0))
    idb_ready = pool.do(lambda e: e.affine_select(out=ident_bf[:], in_=ident_bf[:], compare_op=ALU.not_equal,
                                                  fill=1.0, base=0, pattern=[[-1, P]],
                                                  channel_multiplier=1), zeroed)
    zeroed = pool.do(lambda e: e.memset(causal[:], 0.0))
    causal_ready = pool.do(lambda e: e.affine_select(out=causal[:], in_=causal[:], compare_op=ALU.is_ge,
                                                     fill=NEG, base=0, pattern=[[-1, P]],
                                                     channel_multiplier=1), zeroed)
    consts = []
    one = pool.do(lambda e: e.memset(ones_row[:], 1.0), causal_ready)
    pool.wait(one)
    consts.append(pool.do(lambda e: e.memset(power[:, 0, :], -0.5)))
    consts.append(pool.do(lambda e: e.memset(power[:, 1, :], 0.5)))
    for n in range(NE):
        consts.append(pool.do(lambda e, n=n: e.memset(first_wins[:, :, n:n + 1], float(NE - n))))
    consts.append(dve.do(lambda e: e.memset(eta[:], 1.0)))
    dve.do(lambda e: e.memset(eta[0:1, 0:1], -1.0), consts[-1])
    for i in range(2):
        consts.append(pool.do(lambda e, i=i: e.memset(values[i][:, :, :, HS:VC], 1.0)))
    for i in range(3):
        k_ones = dve.do(lambda e, i=i: e.memset(kstack[i][SROWS:SROWS + MROWS, :, :], 1.0))
    ready = consts[-1]
    for b in pv_bank:
        pv_clear = dve.do(lambda e, b=b: e.memset(b[:], 0.0))
    pv_free = [pv_clear, pv_clear]

    blocks = [(0, 0), (0, 1)]
    for b in range(NB - 2):
        blocks += [(1, b), (0, b + 2)]
    blocks += [(1, NB - 2), (1, NB - 1)]
    NBL = len(blocks)
    NP_ = NBL * NQ

    srcT_ready, values_ready, normT_ready, metric_ready = {}, {}, {}, {}
    srcT_read, values_read = [None, None], [None, None]
    normT_read = metric_read = hid_read = None
    tok_read, acc_ready = [None, None], {}
    stack_in, stackm_in = [sem(f"stack_in{i}") for i in range(3)], [sem(f"stackm_in{i}") for i in range(3)]
    stack_ready, stackm_ready, stack_read = {}, {}, [None, None, None]
    maxes_read = [None, None]
    state = {"parts_read": None, "rest_read": None, "gated_read": None, "turned_read": None,
             "mpart": None, "hid_read": None, "normT_read": None, "metric_read": [None, None],
             "x1": {}, "ffn": None, "experts": [None, None], "gateT_read": None,
             "gate_read": [None, None], "recip": None, "metric_hold": None}
    expert_in = [sem("expert_in0"), sem("expert_in1")]
    heads_out = {}

    def mm(bk, lhsT, rhs, start, stop, *marks, done=False, counter=None):
        return pe.do(lambda e: e.matmul(bk, lhsT, rhs, start=start, stop=stop), *marks,
                     signal=done, done=counter)

    def small_op(lane, fn, *marks):
        return lane.do(fn, *marks)

    def transpose_block(src, src_ready, dst, dst_free):
        last = None
        for t in range(0, TT, 2):
            for i in range(4):
                tile, c = t + i // 2, i % 2
                marks = (free["chain"], src_ready, id_ready, ready) if i == 0 else ()
                m = pe.do(lambda e, i=i, tile=tile, c=c: e.transpose(
                    chain_bank[:, i * P:(i + 1) * P], src[:, tile, c * P:(c + 1) * P], ident[:]),
                    *marks, signal=(i == 3))
            yield True
            view = dst[:, :, t * P:(t + 2) * P].rearrange("p c (t n) -> p t c n", t=2)
            last = act.do(lambda e, view=view: e.copy(view, chain_bank[:].rearrange(
                "p (t c n) -> p t c n", t=2, c=2)), m, *dst_free)
            free["chain"] = last
            yield False
        return last

    def norm_job(bi):
        layer, b = blocks[bi]
        buf = bi % 2
        x, y = acc[buf], tok[buf]
        xin = acc_loaded[bi]
        for t in range(TT):
            m = dve.do(lambda e, t=t: e.bn_stats(stats[:, t, :], x[:, t, :]), xin)
            if t % 2 == 1:
                yield False
        for t in range(TT):
            m2 = dve.do(lambda e, t=t: e.bn_aggr(mv[:, t, :], stats[:, t, :]), m)
        m2 = dve.do(lambda e: e.tensor_scalar(rstd[:], mv[:, :, 1:2].rearrange("p t o -> p (t o)"),
                                              LN_EPS, None, ALU.add), m2)
        r = pool.do(lambda e: e.tensor_tensor(rstd[:], rstd[:], power[:, 0, :], ALU.pow), m2, ready)
        yield False
        for t in range(TT):
            xn = dve.do(lambda e, t=t: e.tensor_scalar(y[:, t, :], x[:, t, :], mv[:, t, 0:1],
                                                       rstd[:, t:t + 1], ALU.subtract, ALU.mult),
                        r, m2, tok_read[buf])
            if t % 2 == 1:
                yield False
        if layer == 0:
            srcT_ready[bi] = yield from transpose_block(y, xn, srcT[buf], (srcT_read[buf],))
            tok_read[buf] = (pe.counter, pe.counter.n)
            return
        normT_ready[bi] = yield from transpose_block(y, xn, normT, (state["normT_read"],))
        turned_all = (pe.counter, pe.counter.n)
        S = lambda i: small[:, i, :]
        for t in range(TT):
            cl = dve.do(lambda e, t=t: e.tensor_scalar(y[:, t, :], y[:, t, :], 8.0, -8.0, ALU.min, ALU.max),
                        turned_all, xn)
            if t % 2 == 1:
                yield False
        for t in range(TT):
            m = dve.do(lambda e, t=t: e.scalar_tensor_tensor(
                out=gated[:, 0:D - 1], in0=y[:, t, 1:D], scalar=1.0, in1=y[:, t, 1:D], op0=ALU.mult,
                op1=ALU.mult, accum_out=small[:, 0, t:t + 1]), cl, state["gated_read"])
            state["gated_read"] = m
            if t % 2 == 1:
                yield False
        m = dve.do(lambda e: e.tensor_scalar(S(1), S(0), 1.0, EPS, ALU.add, ALU.add), m)
        m = pool.do(lambda e: e.tensor_tensor(S(2), S(1), power[:, 1, :], ALU.pow), m)
        yield False
        m = dve.do(lambda e: e.tensor_scalar(S(3), S(2), 1.0 + EPS, None, ALU.max), m)
        m = dve.do(lambda e: e.tensor_scalar(S(4), S(3), 1.0, None, ALU.subtract), m)
        m = dve.do(lambda e: e.scalar_tensor_tensor(out=S(5), in0=S(3), scalar=1.0, in1=S(4),
                                                    op0=ALU.add, op1=ALU.mult), m)
        m = pool.do(lambda e: e.tensor_tensor(S(6), S(5), power[:, 1, :], ALU.pow), m)
        m5 = dve.do(lambda e: e.tensor_tensor(S(7), S(2), S(3), ALU.subtract), m)
        yield False
        m = dve.do(lambda e: e.tensor_tensor(S(6), S(6), S(3), ALU.add), m)
        ln = act.do(lambda e: e.activation(S(8), S(6), ACT.Ln), m)
        m = dve.do(lambda e: e.tensor_tensor(S(9), S(7), S(7), ALU.mult), m5)
        m = dve.do(lambda e: e.tensor_tensor(S(9), S(0), S(9), ALU.subtract), m)
        m = dve.do(lambda e: e.tensor_scalar(S(9), S(9), EPS, None, ALU.max), m)
        m = pool.do(lambda e: e.tensor_tensor(S(10), S(9), power[:, 1, :], ALU.pow), m)
        yield False
        m = dve.do(lambda e: e.tensor_scalar(S(10), S(10), EPS, None, ALU.add), m)
        m = dve.do(lambda e: e.reciprocal(S(10), S(10)), m)
        m = dve.do(lambda e: e.scalar_tensor_tensor(out=S(11), in0=S(8), scalar=1e-3, in1=S(10),
                                                    op0=ALU.max, op1=ALU.mult), m, ln)
        yield False
        for t in range(TT):
            v = dve.do(lambda e, t=t: e.tensor_scalar(y[:, t, 1:D], y[:, t, 1:D], small[:, 11, t:t + 1],
                                                      None, ALU.mult), m)
            if t % 2 == 1:
                yield False
        v = dve.do(lambda e: e.tensor_tensor(y[:, :, 0:1], S(7).rearrange("p (t o) -> p t o", o=1),
                                             S(11).rearrange("p (t o) -> p t o", o=1), ALU.mult), m)
        srcT_ready[bi] = yield from transpose_block(y, v, srcT[buf], (srcT_read[buf],))
        tok_read[buf] = (pe.counter, pe.counter.n)

    def values_job(bi):
        layer, _ = blocks[bi]
        buf = bi % 2
        w = w0v if layer == 0 else w1v
        for t in range(0, TT, 2):
            for i in range(2):
                for c in range(KC):
                    m = mm(chain_bank[:, i * D:(i + 1) * D], srcT[buf][:, c, (t + i) * P:(t + i + 1) * P],
                           w[:, c, :], c == 0, c == KC - 1, free["chain"], srcT_ready[bi], all_weights,
                           done=(i == 1 and c == KC - 1))
            yield True
            view = values[buf][:, t:t + 2, :, 0:HS]
            src = chain_bank[:].rearrange("p (t h d) -> p t h d", t=2, h=H)
            if layer == 0:
                last = dve.do(lambda e, view=view, src=src: e.tensor_tensor(
                    view, src, b0v[:].rearrange("p (o h d) -> p o h d", o=1, h=H).to_broadcast((P, 2, H, HS)), ALU.add),
                    m, values_read[buf], ready, all_weights)
            else:
                last = act.do(lambda e, view=view, src=src: e.copy(view, src), m, values_read[buf], ready)
            free["chain"] = last
            yield False
        values_ready[bi] = last
        srcT_read[buf] = m

    def router_job(bi):
        buf = bi % 2
        G = gate_w[buf]
        for t in range(TT):
            for c in range(KC):
                m = mm(chain_bank[:, t * NE:(t + 1) * NE], srcT[buf][:, c, t * P:(t + 1) * P], rw[:, c, :],
                       c == 0, c == KC - 1, free["chain"], srcT_ready[bi], all_weights,
                       done=(t == TT - 1 and c == KC - 1))
        srcT_read[buf] = m
        yield True
        rb_all = rb[:].rearrange("p (o n) -> p o n", o=1).to_broadcast((P, TT, NE))
        lg = dve.do(lambda e: e.tensor_tensor(logit[:], chain_bank[:, 0:TT * NE].rearrange(
            "p (t n) -> p t n", t=TT), rb_all, ALU.add), m, all_weights)
        free["chain"] = lg
        yield False
        mx = dve.do(lambda e: e.tensor_reduce(lmax[:], logit[:], AX, ALU.max), lg)
        bc = lambda v: v[:].rearrange("p (t o) -> p t o", o=1).to_broadcast((P, TT, NE))
        sh = dve.do(lambda e: e.tensor_tensor(lwork[:], logit[:], bc(lmax), ALU.subtract), mx)
        ex = act.do(lambda e: e.activation(logit[:], lwork[:], ACT.Exp), sh)
        eq = dve.do(lambda e: e.tensor_scalar(lwork[:], lwork[:], 0.0, None, ALU.is_equal), ex)
        eq = dve.do(lambda e: e.tensor_tensor(lwork[:], lwork[:], first_wins[:], ALU.mult), eq, ready)
        fm = dve.do(lambda e: e.tensor_reduce(lmax[:], lwork[:], AX, ALU.max), eq)
        yield False
        oh = dve.do(lambda e: e.tensor_tensor(lwork[:], lwork[:], bc(lmax), ALU.is_equal), fm)
        sm = dve.do(lambda e: e.tensor_reduce(lsum[:], logit[:], AX, ALU.add), ex)
        sm = dve.do(lambda e: e.reciprocal(lsum[:], lsum[:]), sm)
        gw = dve.do(lambda e: e.tensor_tensor(G[:], lwork[:], bc(lsum), ALU.mult), oh, sm, state["gate_read"][buf])
        state["gate_ready", bi] = gw
        yield False

    def experts_job(bi):
        buf = bi % 2
        for ex in range(NE):
            s = ex % 2
            win = load(w_expert[s][:], a["expert_w"][ex], expert_in[s], state["experts"][s])
            for t in range(0, TT, 2):
                for i in range(2):
                    for c in range(KC):
                        m = mm(bulk_bank[:, i * D:(i + 1) * D], srcT[buf][:, c, (t + i) * P:(t + i + 1) * P],
                               w_expert[s][:, c, :], c == 0, c == KC - 1, free["bulk"], win,
                               srcT_ready[bi], done=(i == 1 and c == KC - 1))
                state["experts"][s] = m
                yield True
                for i in range(2):
                    key = ("moe", bi, t + i)
                    last = dve.do(lambda e, i=i, t=t, ex=ex: e.scalar_tensor_tensor(
                        out=acc[buf][:, t + i, :], in0=bulk_bank[:, i * D:(i + 1) * D],
                        scalar=gate_w[buf][:, t + i, ex:ex + 1], in1=acc[buf][:, t + i, :],
                        op0=ALU.mult, op1=ALU.add), m, state["gate_ready", bi], state.get(key))
                    state[key] = last
                free["bulk"] = last
                yield False
        srcT_read[buf] = m
        acc_ready[bi] = last

    def quad_job(n):
        bi, quad = divmod(n, NQ)
        layer, _ = blocks[bi]
        buf, slot = bi % 2, n % 3
        w = w0qk if layer == 0 else w1qk
        q0 = 0 if quad % 2 == 0 else 64
        k0 = 64 - q0
        for half in range(2):
            cols = slice(half * HALF, (half + 1) * HALF)
            for c in range(KC):
                m = mm(chain_bank[:], w[:, c, quad, :], srcT[buf][:, c, cols], c == 0, c == KC - 1,
                       free["chain"], srcT_ready[bi], all_weights, done=(c == KC - 1))
            yield True
            if layer == 0:
                bias = b0qk[:, quad:quad + 1]
                hi = act.do(lambda e, cols=cols, bias=bias: e.activation(
                    part[0][:, cols], chain_bank[:], ACT.Identity, bias=bias), m, state["parts_read"], all_weights)
                r = dve.do(lambda e, cols=cols, bias=bias: e.scalar_tensor_tensor(
                    out=rest[:], in0=chain_bank[:], scalar=bias, in1=part[0][:, cols],
                    op0=ALU.add, op1=ALU.subtract), hi, state["rest_read"])
                free["chain"] = r
            else:
                g = metric[q0:q0 + 64, quad // 2, cols]
                a1 = dve.do(lambda e, g=g: e.tensor_tensor(gated[q0:q0 + 64, :], chain_bank[q0:q0 + 64, :], g,
                                                           ALU.mult), m, metric_ready[bi, quad // 2], state["gated_read"])
                a2 = act.do(lambda e: e.copy(gated[k0:k0 + 64, :], chain_bank[k0:k0 + 64, :]), m, state["gated_read"])
                state["metric_read"][quad // 2] = a1
                pe.wait(a1)
                free["chain"] = a2
                hi = dve.do(lambda e, cols=cols: e.tensor_copy(part[0][:, cols], gated[:]), a1, a2, state["parts_read"])
                r = pool.do(lambda e, cols=cols: e.tensor_tensor(rest[:], gated[:], part[0][:, cols], ALU.subtract),
                            hi, state["rest_read"])
                state["gated_read"] = r
            mid = pool.do(lambda e, cols=cols: e.tensor_scalar(part[1][:, cols], rest[:], 1.0, 0.0, ALU.mult, ALU.add),
                          r, state["parts_read"])
            lo = pool.do(lambda e, cols=cols: e.tensor_tensor(part[2][:, cols], rest[:], part[1][:, cols], ALU.subtract),
                         mid, state["parts_read"])
            state["rest_read"] = lo
            yield False
        srcT_read[buf] = m
        for i, (pq, pk) in enumerate(zip(Q_ORDER, K_ORDER)):
            rows = slice(i * BLK, (i + 1) * BLK)
            load(qstack[slot][rows, :, :], part[pq][q0:q0 + 64, :], stack_in[slot], hi, lo, stack_read[slot])
            mark = load(kstack[slot][rows, :, :], part[pk][k0:k0 + 64, :], stack_in[slot])
        stack_ready[n] = mark
        state["parts_read"] = mark
        yield False

    def metric_job(bi):
        hidden = hid[:].rearrange("p (m n) -> p m n", m=MT)
        for half in range(2):
            cols = slice(half * HALF, (half + 1) * HALF)
            for mt in range(MT):
                for c in range(KC):
                    m = mm(bulk_bank[:], wm1[:, c, mt * P:(mt + 1) * P], normT[:, c, cols], c == 0, c == KC - 1,
                           free["bulk"], normT_ready[bi], all_weights, done=(c == KC - 1))
                yield True
                th = act.do(lambda e, mt=mt: e.activation(hidden[:, mt, :], bulk_bank[:], ACT.Tanh,
                                                          bias=bm1[:, mt:mt + 1]), m, state["hid_read"], state["bm1_ready"])
                free["bulk"] = th
                yield False
            for pair in range(2):
                for kt in range(MT):
                    m = mm(bulk_bank[:], wm2[:, kt, pair, :], hidden[:, kt, :], kt == 0, kt == MT - 1,
                           free["bulk"], th, done=(kt == MT - 1))
                yield True
                g = metric[:, pair, cols]
                t2 = act.do(lambda e, g=g, pair=pair: e.activation(g, bulk_bank[:], ACT.Tanh, bias=bm2[:, pair:pair + 1]),
                            m, state["metric_read"][pair], state["metric_hold"])
                free["bulk"] = t2
                metric_ready[bi, pair] = dve.do(lambda e, g=g, pair=pair: e.tensor_scalar(
                    g, g, 0.1, eta[:, pair:pair + 1], ALU.mult, ALU.add), t2, ready)
                yield False
            state["hid_read"] = m
        state["normT_read"] = m

    def ffn_job(bi, quarters):
        buf = bi % 2
        Q = T // 4
        hidden = hid[:].rearrange("p (h n) -> p h n", h=HT)
        for q in quarters:
            cols = slice(q * Q, (q + 1) * Q)
            for ht in range(0, HT, 2):
                for i in range(2):
                    for c in range(KC):
                        m = mm(bulk_bank[:, i * Q:(i + 1) * Q], wexp[:, c, (ht + i) * P:(ht + i + 1) * P],
                               normT[:, c, cols], c == 0, c == KC - 1, free["bulk"], normT_ready[bi],
                               state["ffn_ready"], state["ffn_ready2"], done=(i == 1 and c == KC - 1))
                yield True
                ev = dve.do(lambda e, ht=ht: e.tensor_tensor(
                    hidden[:, ht:ht + 2, :], bulk_bank[:].rearrange("p (h n) -> p h n", h=2),
                    bexp[:, ht:ht + 2].rearrange("p (h o) -> p h o", o=1).to_broadcast((P, 2, Q)), ALU.add),
                    m, state["hid_read"], state["ffn_bias"])
                free["bulk"] = ev
                yield False
            state["normT_read"] = m
            ge = act.do(lambda e: e.activation(hid[:], hid[:], ACT.Gelu), ev)
            yield False
            for i in range(2):
                for ht in range(HT):
                    m = mm(bulk_bank[:, i * D:(i + 1) * D], hidden[:, ht, i * P:(i + 1) * P], wcon[:, ht, :],
                           ht == 0, False, free["bulk"], ge)
                m = mm(bulk_bank[:, i * D:(i + 1) * D], ones_row[:], bcon[:], False, True, state["bcon_ready"],
                       ready, done=(i == 1))
            state["hid_read"] = m
            yield True
            view = acc[buf][:, 2 * q:2 * q + 2, :]
            last = dve.do(lambda e, view=view: e.tensor_tensor(view, bulk_bank[:].rearrange("p (t d) -> p t d", t=2),
                                                               view, ALU.add), m, acc_loaded[bi])
            free["bulk"] = last
            yield False
        acc_ready[bi] = last

    def butterfly_job():
        bw_in = sem("butterfly_in")
        temp = [None]
        done = all_weights
        wread = None
        for stage in range(STAGES):
            s = 2 ** stage
            win = load(bf_w, a["up"][stage].rearrange("(o c) j -> o c j", o=1).to_broadcast((P, 4, FH // 2)),
                       bw_in, wread)
            for tile in range(KC + 1):
                p = P if tile < KC else 1
                y = (wexp[:, tile, :] if tile < KC else bias_row).rearrange("p (n a s) -> p n a s", a=2, s=s)
                done, wread = yield from butterfly_stage(p, y, s, (0, 1, 2, 3), win, done, wread)
        state["ffn_ready"] = done
        for ht in range(HT):
            m = pe.do(lambda e, ht=ht: e.transpose(chain_bank[:, ht:ht + 1], bias_row[0:1, ht * P:(ht + 1) * P],
                                                   ident[0:1, 0:1]), free["chain"], state["ffn_ready"],
                      signal=(ht == HT - 1))
        yield True
        state["ffn_bias"] = dve.do(lambda e: e.tensor_tensor(bexp[:], chain_bank[:, 0:HT], upb[:], ALU.add), m, all_weights)
        free["chain"] = state["ffn_bias"]
        state["bcon_ready"] = dve.do(lambda e: e.tensor_tensor(bcon[:], bcon[:], dbias, ALU.add), all_weights)
        wt_in = sem("wcon_in")
        held = [normT[:, i, :] for i in range(KC)]
        for i in range(KC):
            dn = load(held[i], a["wconT"][i * P:(i + 1) * P, :], wt_in, m, state["bcon_ready"])
        done_t = dn
        for stage in reversed(range(STAGES)):
            s = 2 ** stage
            win = load(bf_w, a["down"][stage].rearrange("(o c) j -> o c j", o=1).to_broadcast((P, 4, FH // 2)),
                       bw_in, wread)
            for tile in range(KC):
                y = held[tile].rearrange("p (n a s) -> p n a s", a=2, s=s)
                done_t, wread = yield from butterfly_stage(P, y, s, (0, 2, 1, 3), win, done_t, wread)
        for ht in range(0, HT, 2):
            for i in range(2):
                for tile in range(KC):
                    m = pe.do(lambda e, i=i, tile=tile, ht=ht: e.transpose(
                        chain_bank[:, (i * 2 + tile) * P:(i * 2 + tile + 1) * P],
                        held[tile][:, (ht + i) * P:(ht + i + 1) * P], ident[:]), free["chain"], done_t, dn, id_ready,
                        signal=(i == 1 and tile == 1))
            yield True
            last = act.do(lambda e, ht=ht: e.copy(wcon[:, ht:ht + 2, :], chain_bank[:].rearrange("p (h d) -> p h d", h=2)), m)
            free["chain"] = last
            yield False
        state["normT_read"] = m
        state["ffn_ready2"] = last
        state["bm1_ready"] = dve.do(lambda e: e.tensor_tensor(bm1[:], bm1[:], wm1c[:], ALU.subtract), all_weights)
        state["hid_read"] = wread
        state["metric_hold"] = wread
        yield False

    def butterfly_stage(p, y, s, order, win, ydone, wread):
        va, vb = y[:, :, 0, :], y[:, :, 1, :]
        sh = lambda v: v.rearrange("p (n s) -> p n s", s=s)
        for i, src in enumerate((va, vb, va, vb)):
            m = pool.do(lambda e, i=i, src=src: e.tensor_tensor(sh(bf_t[0:p, i, :]), src, sh(bf_w[0:p, order[i], :]),
                                                                ALU.mult), win, ydone, wread)
            if i % 2 == 1:
                yield False
        r = pool.do(lambda e: e.tensor_tensor(va, sh(bf_t[0:p, 0, :]), sh(bf_t[0:p, 1, :]), ALU.add), m)
        r = pool.do(lambda e: e.tensor_tensor(vb, sh(bf_t[0:p, 2, :]), sh(bf_t[0:p, 3, :]), ALU.add), m)
        yield False
        return r, r

    def load_job(bi):
        layer, b = blocks[bi]
        buf = bi % 2
        src = x_dram[b] if layer == 0 else x1_dram[b]
        acc_loaded[bi] = load(acc[buf][:], src, x_in[buf], state.get(("stored", buf)),
                              state["x1"].get(b) if layer == 1 else None)
        yield False

    def finish_job(bi):
        layer, b = blocks[bi]
        buf = bi % 2
        O = tok[buf]
        w = w0o if layer == 0 else w1o
        for half in range(2 if layer == 0 else 0):
            for i in range(4):
                m = pe.do(lambda e, i=i, t=half * 4 + i: e.transpose(
                    chain_bank[0:NE, i * P:(i + 1) * P], gate_w[buf][:, t, :], ident[:]),
                    free["chain"], state["gate_ready", bi], id_ready, signal=(i == 3))
            state["gate_read"][buf] = m
            yield True
            gates = dve.do(lambda e, half=half: e.tensor_copy(gateT[:, half * HALF:(half + 1) * HALF],
                                                              chain_bank[0:NE, :]), m, state["gateT_read"])
            free["chain"] = gates
            yield False
        for t in range(0, TT, 2):
            for i in range(4):
                m = pe.do(lambda e, i=i, t=t: e.transpose(
                    chain_bank[:, i * P:(i + 1) * P], O[:, t + i // 2, (i % 2) * P:(i % 2 + 1) * P], ident[:]),
                    free["chain"], heads_out[bi], signal=(i == 3))
            tok_read[buf] = m
            yield True
            ev = act.do(lambda e: e.copy(turned[:], chain_bank[:]), m, state["turned_read"])
            free["chain"] = ev
            yield True
            for i in range(2):
                for c in range(KC):
                    last = layer == 1 and c == KC - 1
                    m = mm(chain_bank[:, i * D:(i + 1) * D], turned[:, (2 * i + c) * P:(2 * i + c + 1) * P], w[:, c, :],
                           c == 0, last, ev, free["chain"], done=(last and i == 1))
                if layer == 0:
                    mm(chain_bank[:, i * D:(i + 1) * D], ones_row[:], b0o[:], False, False, ready)
                    m = mm(chain_bank[:, i * D:(i + 1) * D], gateT[:, (t + i) * P:(t + i + 1) * P], expert_b[:],
                           False, True, gates, done=(i == 1))
            state["turned_read"] = m
            yield True
            view = acc[buf][:, t:t + 2, :]
            pv = chain_bank[:].rearrange("p (t d) -> p t d", t=2)
            if layer == 0:
                last = dve.do(lambda e, view=view, pv=pv: e.tensor_tensor(view, pv, view, ALU.add), m, acc_ready[bi])
                free["chain"] = last
            else:
                g2 = gated[:].rearrange("p (t d) -> p t d", t=2)
                z = dve.do(lambda e: e.tensor_scalar(gated[:], chain_bank[:], 0.1, 8.0, ALU.mult, ALU.min), m, state["gated_read"])
                free["chain"] = z
                z = dve.do(lambda e: e.tensor_scalar(gated[:], gated[:], -8.0, None, ALU.max), z)
                for i in range(2):
                    sq = dve.do(lambda e, i=i: e.scalar_tensor_tensor(
                        out=rest[:, 0:D - 1], in0=g2[:, i, 1:D], scalar=1.0, in1=g2[:, i, 1:D], op0=ALU.mult,
                        op1=ALU.mult, accum_out=zsum[:, i:i + 1]), z, state["rest_read"])
                    state["rest_read"] = sq
                sq = dve.do(lambda e: e.tensor_scalar(zsum[:], zsum[:], 1.0, EPS, ALU.add, ALU.add), sq)
                x0 = pool.do(lambda e: e.tensor_tensor(g2[:, :, 0:1], zsum[:].rearrange("p (t o) -> p t o", o=1),
                                                       power[:, 1, 0:2].rearrange("p (t o) -> p t o", o=1), ALU.pow), sq, z)
                yield True
                last = dve.do(lambda e, view=view, g2=g2: e.tensor_tensor(view, g2, view, ALU.add), x0, acc_ready[bi])
                state["gated_read"] = last
            dst = x1_dram[b] if layer == 0 else out_dram[b]
            store = sp.do(lambda e, view=view, dst=dst, t=t: e.dma_start(dst[:, t:t + 2, :], view), last,
                          done=acc_out[buf], by=16)
            yield False
        if layer == 0:
            state["gateT_read"] = m
        state[("stored", buf)] = store
        if layer == 0:
            state["x1"][b] = store

    zsum = sb("zsum", [P, 2])

    def heads_job(n, hq, bank_i, pv_mark, srt):
        bi, quad = divmod(n, NQ)
        O = tok[bi % 2]
        ev = act.do(lambda e: e.copy(turned[:], pv_bank[bank_i][:]), pv_mark, state["turned_read"])
        pv_free[bank_i] = ev
        for i in range(4):
            m = pe.do(lambda e, i=i: e.transpose(chain_bank[:, i * P:(i + 1) * P], turned[:, i * P:(i + 1) * P], ident[:]),
                      free["chain"], ev, signal=(i == 3))
        state["turned_read"] = m
        yield True
        bk = chain_bank[:].rearrange("p (t h r) -> p t h r", t=4, h=QH)
        rc = dve.do(lambda e: e.reciprocal(recip[:].rearrange("p t (h o) -> p t h o", o=1), bk[:, :, :, HS:HS + 1]),
                    m, state["recip"])
        dst = O[:, hq * 4:hq * 4 + 4, quad * 64:(quad + 1) * 64].rearrange("p t (h d) -> p t h d", h=QH)
        last = dve.do(lambda e: e.tensor_tensor(dst, bk[:, :, :, 0:HS], recip[:].rearrange(
            "p t (h o) -> p t h o", o=1).to_broadcast((P, 4, QH, HS)), ALU.mult), rc, tok_read[bi % 2])
        state["recip"] = last
        free["chain"] = last
        heads_out[bi] = last
        yield False

    def maxes_job(n):
        slot, mb = n % 3, n % 2
        M = maxes[mb]
        m = dve.do(lambda e: e.tensor_tensor(negmax[:].rearrange("p (h t) -> p h t", h=QH), M[:, 0, :, :],
                                             M[:, 1, :, :], ALU.min), (dve_max, dve_max.n), state.get("negmax_read"))
        maxes_read[mb] = m
        m = pe.do(lambda e: e.transpose(chain_bank[0:QH * TT, 0:P], negmax[:], ident[:]), m, free["chain"])
        state["negmax_read"] = m
        yield True
        mp = mpart[mb]
        src = chain_bank[0:QH * TT, 0:P]
        h = dve.do(lambda e: e.tensor_copy(mp[:, 0, :], src), m, state["mpart"])
        r = dve.do(lambda e: e.tensor_tensor(mrest[:], src, mp[:, 0, :], ALU.subtract), h)
        free["chain"] = r
        md = dve.do(lambda e: e.tensor_copy(mp[:, 1, :], mrest[:]), r)
        lo = dve.do(lambda e: e.tensor_tensor(mp[:, 2, :], mrest[:], mp[:, 1, :], ALU.subtract), md)
        for i in range(3):
            mark = load(qstack[slot][SROWS + i:SROWS + i + 1, :, :], mp[:, i, :], stackm_in[slot], lo, stack_read[slot])
        stackm_ready[n] = mark
        state["mpart"] = mark
        yield False

    def first_pass(n):
        bi, _ = divmod(n, NQ)
        layer, _ = blocks[bi]
        slot, M = n % 3, maxes[n % 2]
        pe.wait(k_ones)
        if layer == 0:
            dve.do(lambda e: e.memset(M[:, 1, :, 0:4], BIG), maxes_read[n % 2], done=dve_max)
        for j in range(QH):
            for t in range(TT):
                for half in range(2):
                    width = HALF
                    if layer == 0:
                        width = min(HALF, (t + 1) * P - half * HALF)
                        if width <= 0:
                            continue
                    i = first_pass.count % 2
                    first_pass.count += 1
                    bk = max_bank[i]
                    diag = layer == 0 and half == t // 4
                    m = mm(bk[:, 0:width], qstack[slot][0:SROWS, j, t * P:(t + 1) * P],
                           kstack[slot][0:SROWS, j, half * HALF:half * HALF + width], True, not diag,
                           stack_ready[n], max_free[i], done=not diag, counter=pe_max)
                    if diag:
                        m = mm(bk[:, width - P:width], ident_bf[:], causal[:], False, True, causal_ready,
                               done=True, counter=pe_max)
                    max_free[i] = dve.do(lambda e, bk=bk, width=width, half=half, j=j, t=t: e.tensor_reduce(
                        M[:, half, j, t:t + 1], bk[:, 0:width], AX, ALU.max, negate=True), m, maxes_read[n % 2],
                        done=dve_max)
                    yield
    first_pass.count = 0

    def second_pass(n):
        bi, quad = divmod(n, NQ)
        layer, _ = blocks[bi]
        slot, V = n % 3, values[bi % 2]
        pending = None
        def product(hq, kt, nk, c0, pb, masked):
            for j in range(QH):
                m = pe.do(lambda e, j=j: e.matmul(pv_bank[hq][32 * j:32 * j + VC, c0:HALF], V[:, kt, 4 * quad + j, :],
                                                  prob[pb][:, j, c0:HALF], start=(kt == 0), stop=(kt == nk - 1)),
                          masked, values_ready[bi], pv_free[hq] if kt == 0 else None, signal=(j == QH - 1))
            second_pass.read[pb] = m
            return m
        for hq in range(2):
            nk = TT if layer == 1 or hq == 1 else 4
            for kt in range(nk):
                c0 = max(0, kt * P - hq * HALF) if layer == 0 else 0
                pb = second_pass.count % 2
                second_pass.count += 1
                for j in range(QH):
                    i = j % 2
                    m = mm(score_bank[i][:, c0:HALF], kstack[slot][0:SROWS + MROWS, j, kt * P:(kt + 1) * P],
                           qstack[slot][0:SROWS + MROWS, j, hq * HALF + c0:(hq + 1) * HALF], True, True,
                           score_free[i], stack_ready[n], stackm_ready[n], done=True, counter=pe_scores)
                    e_ = act.do(lambda e, i=i, j=j, c0=c0, pb=pb: e.activation(prob[pb][:, j, c0:HALF],
                                score_bank[i][:, c0:HALF], ACT.Exp, scale=SCALE), m, second_pass.read[pb], done=act_exp)
                    score_free[i] = e_
                masked = e_
                if layer == 0 and kt * P >= hq * HALF:
                    view = prob[pb][:, :, c0:c0 + P]
                    masked = pool.do(lambda e, view=view: e.affine_select(
                        out=view, in_=view, compare_op=ALU.is_ge, fill=0.0, base=0,
                        pattern=[[0, QH], [1, P]], channel_multiplier=-1), e_)
                if pending:
                    product(*pending)
                pending = (hq, kt, nk, c0, pb, masked)
                if kt == nk - 1:
                    stack_read[slot] = (pe_scores, pe_scores.n)
                yield None
                if kt == nk - 1:
                    m = product(*pending)
                    pending = None
                    values_read[bi % 2] = m
                    yield ("out", n, hq, m)
    second_pass.count, second_pass.read = 0, [None, None]

    class Stream:

        def __init__(self):
            self.jobs, self.urgent, self.held, self.now = [], [], False, None

        def step(self):
            if self.now is None or (not self.held and self.urgent and not self.now[1]):
                if self.urgent:
                    if self.now is not None:
                        self.jobs.insert(0, self.now[0])
                    self.now = (self.urgent.pop(0), True)
                elif self.jobs:
                    self.now = (self.jobs.pop(0), False)
                else:
                    return False
            try:
                self.held = next(self.now[0])
            except StopIteration:
                self.now, self.held = None, False
            return True

        def empty(self):
            return self.now is None and not self.jobs and not self.urgent

        def drain(self):
            while not self.empty():
                self.step()

    chain, bulk = Stream(), Stream()

    def jobs_of(period):
        cj, bj, cs, bs = [], [], 0, 0
        bi, q = divmod(period, NQ)
        if q == 0 and bi >= 1:
            cj.append(finish_job(bi - 1)); cs += 20
            if bi + 1 < NBL and period > 0:
                cj.append(load_job(bi + 1))
        if 0 <= period + 2 < NP_:
            cj.append(quad_job(period + 2)); cs += 7
        nb = bi + 1
        if q == 1 and nb < NBL:
            cj.append(norm_job(nb)); cs += 20 if blocks[nb][0] == 0 else 50
            cj.append(values_job(nb)); cs += 10
            if blocks[nb][0] == 0:
                cj.append(router_job(nb)); cs += 8
        if nb < NBL and q in (2, 3):
            if blocks[nb][0] == 1 and q == 2:
                bj.append(ffn_job(nb, (0,))); bs += 12
            if blocks[nb][0] == 1 and q == 3:
                bj.append(ffn_job(nb, (1,))); bs += 12
        if q == 0 and blocks[bi][0] == 1:
            soon = bi + 1 < NBL and blocks[bi + 1][0] == 1
            bj.append(ffn_job(bi, (2, 3) if soon else (2,))); bs += 24 if soon else 12
        if q == 1 and blocks[bi][0] == 1 and not (bi + 1 < NBL and blocks[bi + 1][0] == 1):
            bj.append(ffn_job(bi, (3,))); bs += 12
        return cj, bj, cs, bs

    def run_all(*jobs):
        for g in jobs:
            for _ in g:
                pass

    run_all(norm_job(0), values_job(0), router_job(0), quad_job(0), quad_job(1))
    blk = load_job(1); run_all(blk)
    for _ in first_pass(0):
        pass
    run_all(maxes_job(0))

    experts = {bi: experts_job(bi) for bi in range(NBL) if blocks[bi][0] == 0}
    butter = butterfly_job()
    for period in range(NP_):
        bi, q = divmod(period, NQ)
        cj, bj, cs, bs = jobs_of(period)
        chain.jobs += cj
        nb = bi + 1
        if q == 1 and nb < NBL and blocks[nb][0] == 1:
            pass
        bulk.jobs += bj
        if q == 0 and blocks[bi][0] == 0 or (q == 1 and blocks[bi][0] == 0):
            pass
        ex_steps = 0
        ex_gen = None
        cand = nb if q in (2, 3) else bi
        if cand < NBL and blocks[cand][0] == 0 and cand in experts:
            ex_gen = experts[cand]
            left = (4 if q == 2 else 3 if q == 3 else 2 if q == 0 else 1)
            if cand == 0:
                left = 2 if q == 0 else 1
            ex_steps = {4: 16, 3: 16, 2: 16, 1: 200}[left] if cand else (32 if left == 2 else 200)
            bs += min(ex_steps, 32)
        atten = second_pass(period)
        first = first_pass(period + 1) if period + 1 < NP_ else iter(())
        layer = blocks[bi][0]
        n_steps = 16 if layer == 1 else 12
        next_layer = blocks[(period + 1) // NQ][0] if period + 1 < NP_ else 1
        n_first = (64 if next_layer == 1 else 48)
        done_first = done_c = done_b = 0
        k = 0
        bfly_left = 40 if butter is not None and period < 4 else 0
        for ev in atten:
            if ev is not None:
                chain.urgent.append(heads_job(ev[1], ev[2], ev[2], ev[3], None))
                continue
            k += 1
            frac = k / n_steps
            while done_first < n_first * frac:
                done_first += 1
                next(first, None)
                if done_first % 2:
                    continue
            while done_c < cs * frac:
                done_c += 1
                chain.step()
            while chain.urgent and not chain.held:
                chain.step()
            while done_b < bs * frac:
                done_b += 1
                if ex_gen is not None and ex_steps > 0:
                    ex_steps -= 1
                    if next(ex_gen, "end") == "end":
                        ex_gen = None
                elif not bulk.step():
                    break
            if butter is not None:
                for _ in range(3):
                    if chain.held:
                        break
                    held = next(butter, "end")
                    while held is True:
                        held = next(butter, "end")
                    if held == "end":
                        butter = None
                        break
        for _ in first:
            pass
        chain.drain()
        if period == NQ and butter is not None:
            run_all(butter)
            butter = None
        if ex_gen is not None:
            while ex_steps > 0 and next(ex_gen, "end") != "end":
                ex_steps -= 1
        bulk.drain()
        if q == 1 and nb < NBL and blocks[nb][0] == 1:
            run_all(metric_job(nb))
        if period + 1 < NP_:
            run_all(maxes_job(period + 1))
    run_all(finish_job(NBL - 1))
    for c in acc_out:
        sp.wait((c, c.n))

    with nc.Block() as block:
        block.sync(sp.run)
        block.tensor(pe.run)
        block.scalar(act.run)
        block.vector(dve.run)
        block.gpsimd(pool.run)


def build(nc, aps, out):
    with ExitStack() as ctx:
        two_layers(nc, ctx, aps, out)


def kernel(**inputs):
    import concourse.bacc as bacc
    from concourse.bass_utils import run_bass_kernel_spmd

    g = {k: np.asarray(v) for k, v in inputs.items()}

    def rows(w):
        return w.reshape(w.shape[0] // P, P, -1).transpose(1, 0, 2)

    def quad_cols(w):
        w = w.reshape(*w.shape[:-1], NQ, QH, HS)
        return np.swapaxes(w, -1, -2).reshape(*w.shape[:-3], NQ, QH * HS)

    def qk_cols(q, k):
        q, k = quad_cols(q), quad_cols(k)
        even = np.concatenate([q, k], -1)
        odd = np.concatenate([k, q], -1)
        pick = [even[..., i, :] if i % 2 == 0 else odd[..., i, :] for i in range(NQ)]
        return np.stack(pick, -2)

    w0 = g["L0_attn_attn_W"].reshape(D, H, 3, HS)
    b0 = g["L0_attn_attn_b"].reshape(H, 3, HS)
    flat = lambda w: w.reshape(*w.shape[:-2], H * HS)
    w2q = quad_cols(g["L1_attn_W2"].T)
    b2q = quad_cols(g["L1_attn_b2"])
    host = {
        "x": g["L0_attn_encodings"],
        "w0qk": rows(qk_cols(flat(w0[:, :, 0]), flat(w0[:, :, 1])).reshape(D, NQ * P)).reshape(P, KC, NQ, P),
        "b0qk": qk_cols(flat(b0[:, 0]), flat(b0[:, 1])).T,
        "w0v": rows(flat(w0[:, :, 2])),
        "b0v": flat(b0[:, 2]),
        "w0o": rows(g["L0_attn_out_W"]),
        "b0o": g["L0_attn_out_b"][None, :],
        "rw": rows(g["L0_ffn_router_w"]),
        "rb": g["L0_ffn_router_b"],
        "expert_w": g["L0_ffn_expert_w"].reshape(NE, KC, P, D).transpose(0, 2, 1, 3),
        "expert_b": g["L0_ffn_expert_b"],
        "w1qk": rows(qk_cols(g["L1_attn_Wq"].T, g["L1_attn_Wk"].T).reshape(D, NQ * P)).reshape(P, KC, NQ, P),
        "w1v": rows(g["L1_attn_Wv"].T),
        "w1o": rows(g["L1_attn_Wo"].T),
        "wm1": rows(g["L1_attn_W1"].T),
        "bm1": g["L1_attn_b1"].reshape(MT, P).T,
        "wm1c": g["L1_attn_W1"][:, 0].reshape(MT, P).T,
        "wm2": w2q.reshape(MT, P, 2, P).transpose(1, 0, 2, 3),
        "bm2": b2q.reshape(2, P).T,
        "wexp": rows(g["L1_ffn_W_exp"]),
        "b_exp": g["L1_ffn_b_exp"][None, :],
        "upb": g["L1_ffn_up_bias"].reshape(HT, P).T,
        "up": g["L1_ffn_up_weights"].reshape(STAGES, FH // 2, 4).transpose(0, 2, 1),
        "down": g["L1_ffn_down_weights"].reshape(STAGES, FH // 2, 4).transpose(0, 2, 1),
        "wconT": g["L1_ffn_W_con"].T,
        "b_con": g["L1_ffn_b_con"][None, :],
        "down_bias": g["L1_ffn_down_bias"][None, :],
    }
    nc = bacc.Bacc("TRN2", target_bir_lowering=False, num_devices=1, dynamic_dma_scratch_size=1024)
    arrays, aps = {}, {}
    for name, v in host.items():
        v = np.ascontiguousarray(v)
        arrays["in_" + name] = v
        aps[name] = nc.dram_tensor("in_" + name, v.shape, mybir.dt.from_np(v.dtype), kind="ExternalInput").ap()
    out = nc.dram_tensor("out", (NB, T, D), F32, kind="ExternalOutput").ap()
    build(nc, aps, out)
    r = run_bass_kernel_spmd(nc, [arrays], core_ids=[0])
    return r.results[0]["out"]
```

```python
from contextlib import ExitStack

import numpy as np

import concourse.bass as bass
from concourse import mybir

F32 = mybir.dt.float32
BF16 = mybir.dt.bfloat16
ALU = mybir.AluOpType
ACT = mybir.ActivationFunctionType
AX = mybir.AxisListType.X

P = 128
NB, T, D = 8, 1024, 256
H, HS = 16, 16
QH = 4
NQ = H // QH
TT = T // P
KC = D // P
NE = 8
FH = 1024
HT = FH // P
MH = 2 * D
MT = MH // P
STAGES = 10
HALF = 512
BLK = HS
Q_ORDER = (0, 0, 1, 0, 2, 1)
K_ORDER = (0, 1, 0, 2, 0, 1)
SROWS = BLK * len(Q_ORDER)
MROWS = 3
SCALE = HS ** -0.5
NEG = -1.0e30
BIG = 3.0e38
VC = HS + 1
LN_EPS = 1e-5
EPS = 1e-6
PACE = {"act": 0.8, "dve": 1.0, "pool": 0.6}
FIRST_AHEAD = 1.5
SLACK = 0.0
BUTTER_RATE = 0.25


class Counter:

    def __init__(self, sem):
        self.sem, self.n, self.when = sem, 0, {}

    def add(self, by, when):
        self.n += by
        self.when[self.n] = when
        return self, self.n


class Lane:
    cost = 0.0
    wake = 0.0

    def __init__(self, name, counter, price, reach):
        self.name, self.counter, self.queue, self.known = name, counter, [], {}
        self.price, self.reach, self.clock = price, reach, 0.0

    def wait(self, *marks):
        for m in marks:
            if m is None:
                continue
            counter, value = m
            if self.known.get(id(counter), 0) < value:
                self.known[id(counter)] = value
                self.clock = max(self.clock, counter.when[value])
                self.queue.append(lambda eng, s=counter.sem, v=value: eng.wait_ge(s, v))

    def do(self, fn, *marks, done=None, by=1, signal=True, price=None):
        self.wait(*marks)
        price = self.price if price is None else price
        Lane.cost += price * PACE.get(self.name, 1.0)
        self.clock += price if self.name != "sp" else 60
        Lane.wake = self.clock + self.reach
        if not signal:
            self.queue.append(lambda eng: fn(eng))
            Lane.wake = 0.0
            return None
        counter = done or self.counter
        mark = counter.add(by, Lane.wake)
        self.queue.append(lambda eng, s=counter.sem: fn(eng).then_inc(s, by))
        return mark

    def run(self, eng):
        for step in self.queue:
            step(eng)


def when(mark):
    return mark[0].when[mark[1]] if mark else 0.0


class Memory:

    def __init__(self, nc, ctx):
        self.nc, self.ctx, self.held = nc, ctx, {}

    def get(self, name, make):
        if name not in self.held:
            self.held[name] = make()
        return self.held[name]


def two_layers(mem, a, out, plan):
    nc, ctx = mem.nc, mem.ctx

    def sb(name, shape, dt=F32):
        return mem.get(name, lambda: ctx.enter_context(nc.sbuf_tensor(name, shape, dt)))

    def bank(name):
        return mem.get(name, lambda: ctx.enter_context(nc.psum_tensor(name, [P, HALF], F32)))

    def sem(name):
        return Counter(mem.get(name, lambda: ctx.enter_context(nc.semaphore(name))))

    pe = Lane("pe", sem("pe_done"), 60, 190)
    act = Lane("act", sem("act_done"), 500, 150)
    dve = Lane("dve", sem("dve_done"), 350, 150)
    pool = Lane("pool", sem("pool_done"), 700, 150)
    sp = Lane("sp", None, 60, 2500)
    pe_scores, pe_max = sem("pe_scores"), sem("pe_max")
    act_exp, dve_max = sem("act_exp"), sem("dve_max")
    weights_in = sem("weights_in")

    def load(dst, src, counter, *marks):
        return sp.do(lambda e: e.dma_start(dst, src), *marks, done=counter, by=16)

    max_bank = [bank("max0"), bank("max1")]
    score_bank = [bank("score0"), bank("score1")]
    pv_bank = bank("pv")
    chain_bank = bank("chain")
    bulk_banks = [bank("bulk0"), bank("bulk1")]
    max_free, score_free = [None, None], [None, None]
    free = {"chain": None, 0: None, 1: None, "pv": None}

    ident, ident_bf = sb("ident", [P, P]), sb("ident_bf", [P, P], BF16)
    causal = sb("causal", [P, P], BF16)
    ones_row = sb("ones_row", [1, P])
    power = sb("power", [P, 2, TT])
    w0qk, b0qk = sb("w0qk", [P, KC, NQ, P]), sb("b0qk", [P, NQ])
    w0v, b0v = sb("w0v", [P, KC, D]), sb("b0v", [P, D])
    w0o, b0o = sb("w0o", [P, KC, D]), sb("b0o", [1, D])
    rw, rb = sb("rw", [P, KC, NE]), sb("rb", [P, NE])
    expert_b = sb("expert_b", [NE, D])
    first_wins = sb("first_wins", [P, TT, NE])
    w1qk, w1v, w1o = sb("w1qk", [P, KC, NQ, P]), sb("w1v", [P, KC, D]), sb("w1o", [P, KC, D])
    wm1, bm1, wm1c = sb("wm1", [P, KC, MH]), sb("bm1", [P, MT]), sb("wm1c", [P, MT])
    wm2, bm2, eta = sb("wm2", [P, MT, 2, P]), sb("bm2", [P, 2]), sb("eta", [P, 2])
    wexp, bexp = sb("wexp", [P, KC, FH]), sb("bexp", [P, HT])
    upb = sb("upb", [P, HT])
    wcon = sb("wcon", [P, HT, D])
    bcon = sb("bcon", [1, D])
    w_expert = [sb(f"w_expert{i}", [P, KC, D]) for i in range(2)]

    qstack = [sb(f"qstack{i}", [P, QH, T], BF16) for i in range(3)]
    kstack = [sb(f"kstack{i}", [P, QH, T], BF16) for i in range(3)]
    values = [sb(f"values{i}", [P, TT, H, VC]) for i in range(2)]
    prob = [sb(f"prob{i}", [P, QH, HALF]) for i in range(2)]
    srcT = [sb(f"srcT{i}", [P, KC, T]) for i in range(2)]
    normT = sb("normT", [P, KC, T])
    acc = [sb(f"acc{i}", [P, TT, D]) for i in range(2)]
    tok = [sb(f"tok{i}", [P, TT, D]) for i in range(2)]
    part = [sb(f"part{i}", [P, T], BF16) for i in range(3)]
    rest, gated = sb("rest", [P, HALF]), sb("gated", [P, HALF])
    hid = sb("hid", [P, 4 * HALF])
    metric = sb("metric", [P, 2, T])
    turned, headsT = sb("turned", [P, HALF]), sb("headsT", [P, HALF])
    maxes = [sb(f"maxes{i}", [P, 2, QH, TT]) for i in range(2)]
    negmax = sb("negmax", [P, QH * TT])
    mrest = sb("mrest", [QH * TT, P])
    mpart = [sb("mpart", [QH * TT, 3, P], BF16)] * 2
    stats, mv = sb("stats", [P, TT, 6]), sb("mv", [P, TT, 2])
    small = sb("small", [P, 12, TT])
    rstd = sb("rstd", [P, TT])
    recip = sb("recip", [P, 4, QH])
    logit = sb("logit", [P, TT, NE])
    lwork = sb("lwork", [P, TT, NE])
    lmax, lsum = sb("lmax", [P, TT]), sb("lsum", [P, TT])
    gate_w = [sb(f"gate_w{i}", [P, TT, NE]) for i in range(2)]
    gateT = sb("gateT", [NE, HALF])
    x1_dram = mem.get("x1", lambda: nc.dram_tensor("x1_scratch", [NB, P, TT, D], F32, kind="Internal").ap())
    bf_w = metric[:, :, :].rearrange("p a b -> p (a b)").rearrange("p (c j) -> p c j", c=4)
    bf_t = hid[:, :].rearrange("p (c j) -> p c j", c=4)
    bias_row, dbias = normT[0:1, 0, :], normT[0:1, 1, 0:D]

    def bcast(ap, n, p=P):
        return ap.rearrange("(o n) -> o n", o=1).to_broadcast((p, n))

    W = {}

    def weight(name, dst, src):
        W[name] = load(dst, src, weights_in)

    x_in = [sem("x_in0"), sem("x_in1")]
    acc_out = [sem("acc_out0"), sem("acc_out1")]
    x_dram = a["x"].rearrange("b (t p) d -> b p t d", p=P, t=TT)
    out_dram = out.rearrange("b (t p) d -> b p t d", p=P, t=TT)
    acc_loaded = {}
    acc_loaded[0] = load(acc[0][:], x_dram[0], x_in[0])
    weight("qk0", w0qk[:], a["w0qk"])
    weight("v0", w0v[:], a["w0v"])
    weight("rw", rw[:], a["rw"])
    weight("b0qk", b0qk[:], a["b0qk"])
    weight("b0v", b0v[:], bcast(a["b0v"], D))
    weight("rb", rb[:], bcast(a["rb"], NE))
    weight("o0", w0o[:], a["w0o"])
    weight("b0o", b0o[:], a["b0o"])
    weight("eb", expert_b[:], a["expert_b"])
    weight("wexp", wexp[:], a["wexp"])
    weight("bexp", bias_row, a["b_exp"])
    weight("upb", upb[:], a["upb"])
    weight("bcon", bcon[:], a["b_con"])
    weight("dbias", dbias, a["down_bias"])
    weight("qk1", w1qk[:], a["w1qk"])
    weight("v1", w1v[:], a["w1v"])
    weight("o1", w1o[:], a["w1o"])
    weight("m1", wm1[:], a["wm1"])
    weight("bm1", bm1[:], a["bm1"])
    weight("m1c", wm1c[:], a["wm1c"])
    weight("m2", wm2[:], a["wm2"])
    weight("bm2", bm2[:], a["bm2"])
    all_weights = (weights_in, weights_in.n)

    zeroed = pool.do(lambda e: e.memset(ident[:], 0.0))
    id_ready = pool.do(lambda e: e.affine_select(out=ident[:], in_=ident[:], compare_op=ALU.not_equal,
                                                 fill=1.0, base=0, pattern=[[-1, P]],
                                                 channel_multiplier=1), zeroed)
    zeroed = pool.do(lambda e: e.memset(ident_bf[:], 0.0))
    idb_ready = pool.do(lambda e: e.affine_select(out=ident_bf[:], in_=ident_bf[:], compare_op=ALU.not_equal,
                                                  fill=1.0, base=0, pattern=[[-1, P]],
                                                  channel_multiplier=1), zeroed)
    zeroed = pool.do(lambda e: e.memset(causal[:], 0.0))
    causal_ready = pool.do(lambda e: e.affine_select(out=causal[:], in_=causal[:], compare_op=ALU.is_ge,
                                                     fill=NEG, base=0, pattern=[[-1, P]],
                                                     channel_multiplier=1), zeroed)
    consts = []
    one = pool.do(lambda e: e.memset(ones_row[:], 1.0), causal_ready)
    pool.wait(one)
    consts.append(pool.do(lambda e: e.memset(power[:, 0, :], -0.5)))
    consts.append(pool.do(lambda e: e.memset(power[:, 1, :], 0.5)))
    for n in range(NE):
        consts.append(pool.do(lambda e, n=n: e.memset(first_wins[:, :, n:n + 1], float(NE - n))))
    consts.append(dve.do(lambda e: e.memset(eta[:], 1.0)))
    dve.do(lambda e: e.memset(eta[0:1, 0:1], -1.0), consts[-1])
    for i in range(2):
        consts.append(pool.do(lambda e, i=i: e.memset(values[i][:, :, :, HS:VC], 1.0)))
    for i in range(3):
        k_ones = dve.do(lambda e, i=i: e.memset(kstack[i][SROWS:SROWS + MROWS, :, :], 1.0))
    ready = consts[-1]
    free["pv"] = dve.do(lambda e: e.memset(pv_bank[:], 0.0))

    blocks = [(0, 0), (0, 1)]
    for b in range(NB - 2):
        blocks += [(1, b), (0, b + 2)]
    blocks += [(1, NB - 2), (1, NB - 1)]
    NBL = len(blocks)
    NP_ = NBL * NQ

    srcT_ready, values_ready, normT_ready, metric_ready = {}, {}, {}, {}
    srcT_read, values_read = [None, None], [None, None]
    normT_read = metric_read = hid_read = None
    tok_read, acc_ready = [None, None], {}
    stack_in, stackm_in = [sem(f"stack_in{i}") for i in range(3)], [sem(f"stackm_in{i}") for i in range(3)]
    stack_ready, stackm_ready, stack_read = {}, {}, [None, None, None]
    maxes_read = [None, None]
    state = {"parts_read": None, "rest_read": None, "gated_read": None, "turned_read": None,
             "mpart": None, "hid_read": None, "normT_read": None, "metric_read": [None, None],
             "x1": {}, "ffn": None, "experts": [None, None], "gateT_read": None,
             "gate_read": [None, None], "recip": None,}
    expert_in = [sem("expert_in0"), sem("expert_in1")]
    heads_out = {}

    def mm(bk, lhsT, rhs, start, stop, *marks, done=False, counter=None):
        n = 1
        for size in rhs.shape[1:]:
            n *= size
        return pe.do(lambda e: e.matmul(bk, lhsT, rhs, start=start, stop=stop), *marks,
                     signal=done, done=counter, price=n * (4 if rhs.dtype == F32 else 1) / 2.4)

    def small_op(lane, fn, *marks):
        return lane.do(fn, *marks)

    def transpose_block(src, src_ready, dst, dst_free):
        last = None
        for t in range(0, TT, 2):
            for i in range(4):
                tile, c = t + i // 2, i % 2
                marks = (free["chain"], src_ready, id_ready, ready) if i == 0 else ()
                m = pe.do(lambda e, i=i, tile=tile, c=c: e.transpose(
                    chain_bank[:, i * P:(i + 1) * P], src[:, tile, c * P:(c + 1) * P], ident[:]),
                    *marks, signal=(i == 3))
            yield True
            view = dst[:, :, t * P:(t + 2) * P].rearrange("p c (t n) -> p t c n", t=2)
            last = act.do(lambda e, view=view: e.copy(view, chain_bank[:].rearrange(
                "p (t c n) -> p t c n", t=2, c=2)), m, *dst_free)
            free["chain"] = last
            yield False
        return last

    def norm_job(bi):
        layer, b = blocks[bi]
        buf = bi % 2
        x, y = acc[buf], tok[buf]
        xin = acc_loaded[bi]
        for t in range(TT):
            m = dve.do(lambda e, t=t: e.bn_stats(stats[:, t, :], x[:, t, :]), xin)
            if t % 2 == 1:
                yield False
        for t in range(TT):
            m2 = dve.do(lambda e, t=t: e.bn_aggr(mv[:, t, :], stats[:, t, :]), m)
        m2 = dve.do(lambda e: e.tensor_scalar(rstd[:], mv[:, :, 1:2].rearrange("p t o -> p (t o)"),
                                              LN_EPS, None, ALU.add), m2)
        r = pool.do(lambda e: e.tensor_tensor(rstd[:], rstd[:], power[:, 0, :], ALU.pow), m2, ready)
        yield False
        for t in range(TT):
            xn = dve.do(lambda e, t=t: e.tensor_scalar(y[:, t, :], x[:, t, :], mv[:, t, 0:1],
                                                       rstd[:, t:t + 1], ALU.subtract, ALU.mult),
                        r, m2, tok_read[buf])
            if t % 2 == 1:
                yield False
        if layer == 0:
            srcT_ready[bi] = yield from transpose_block(y, xn, srcT[buf], (srcT_read[buf],))
            tok_read[buf] = (pe.counter, pe.counter.n)
            return
        normT_ready[bi] = yield from transpose_block(y, xn, normT, (state["normT_read"],))
        turned_all = (pe.counter, pe.counter.n)
        S = lambda i: small[:, i, :]
        for t in range(TT):
            cl = dve.do(lambda e, t=t: e.tensor_scalar(y[:, t, :], y[:, t, :], 8.0, -8.0, ALU.min, ALU.max),
                        turned_all, xn)
            if t % 2 == 1:
                yield False
        for t in range(TT):
            m = dve.do(lambda e, t=t: e.scalar_tensor_tensor(
                out=gated[:, 0:D - 1], in0=y[:, t, 1:D], scalar=1.0, in1=y[:, t, 1:D], op0=ALU.mult,
                op1=ALU.mult, accum_out=small[:, 0, t:t + 1]), cl, state["gated_read"])
            state["gated_read"] = m
            if t % 2 == 1:
                yield False
        m = dve.do(lambda e: e.tensor_scalar(S(1), S(0), 1.0, EPS, ALU.add, ALU.add), m)
        m = pool.do(lambda e: e.tensor_tensor(S(2), S(1), power[:, 1, :], ALU.pow), m)
        yield False
        m = dve.do(lambda e: e.tensor_scalar(S(3), S(2), 1.0 + EPS, None, ALU.max), m)
        m = dve.do(lambda e: e.tensor_scalar(S(4), S(3), 1.0, None, ALU.subtract), m)
        m = dve.do(lambda e: e.scalar_tensor_tensor(out=S(5), in0=S(3), scalar=1.0, in1=S(4),
                                                    op0=ALU.add, op1=ALU.mult), m)
        m = pool.do(lambda e: e.tensor_tensor(S(6), S(5), power[:, 1, :], ALU.pow), m)
        m5 = dve.do(lambda e: e.tensor_tensor(S(7), S(2), S(3), ALU.subtract), m)
        yield False
        m = dve.do(lambda e: e.tensor_tensor(S(6), S(6), S(3), ALU.add), m)
        ln = act.do(lambda e: e.activation(S(8), S(6), ACT.Ln), m)
        m = dve.do(lambda e: e.tensor_tensor(S(9), S(7), S(7), ALU.mult), m5)
        m = dve.do(lambda e: e.tensor_tensor(S(9), S(0), S(9), ALU.subtract), m)
        m = dve.do(lambda e: e.tensor_scalar(S(9), S(9), EPS, None, ALU.max), m)
        m = pool.do(lambda e: e.tensor_tensor(S(10), S(9), power[:, 1, :], ALU.pow), m)
        yield False
        m = dve.do(lambda e: e.tensor_scalar(S(10), S(10), EPS, None, ALU.add), m)
        m = dve.do(lambda e: e.reciprocal(S(10), S(10)), m)
        m = dve.do(lambda e: e.scalar_tensor_tensor(out=S(11), in0=S(8), scalar=1e-3, in1=S(10),
                                                    op0=ALU.max, op1=ALU.mult), m, ln)
        yield False
        for t in range(TT):
            v = dve.do(lambda e, t=t: e.tensor_scalar(y[:, t, 1:D], y[:, t, 1:D], small[:, 11, t:t + 1],
                                                      None, ALU.mult), m)
            if t % 2 == 1:
                yield False
        v = dve.do(lambda e: e.tensor_tensor(y[:, :, 0:1], S(7).rearrange("p (t o) -> p t o", o=1),
                                             S(11).rearrange("p (t o) -> p t o", o=1), ALU.mult), m)
        srcT_ready[bi] = yield from transpose_block(y, v, srcT[buf], (srcT_read[buf],))
        tok_read[buf] = (pe.counter, pe.counter.n)

    def values_job(bi):
        layer, _ = blocks[bi]
        buf = bi % 2
        w = w0v if layer == 0 else w1v
        for t in range(0, TT, 2):
            for i in range(2):
                for c in range(KC):
                    m = mm(chain_bank[:, i * D:(i + 1) * D], srcT[buf][:, c, (t + i) * P:(t + i + 1) * P],
                           w[:, c, :], c == 0, c == KC - 1, free["chain"], srcT_ready[bi], all_weights,
                           done=(i == 1 and c == KC - 1))
                    yield True
            view = values[buf][:, t:t + 2, :, 0:HS]
            src = chain_bank[:].rearrange("p (t h d) -> p t h d", t=2, h=H)
            if layer == 0:
                last = dve.do(lambda e, view=view, src=src: e.tensor_tensor(
                    view, src, b0v[:].rearrange("p (o h d) -> p o h d", o=1, h=H).to_broadcast((P, 2, H, HS)), ALU.add),
                    m, values_read[buf], ready, all_weights)
            else:
                last = act.do(lambda e, view=view, src=src: e.copy(view, src), m, values_read[buf], ready)
            free["chain"] = last
            yield False
        values_ready[bi] = last
        srcT_read[buf] = m

    def router_job(bi):
        buf = bi % 2
        G = gate_w[buf]
        for t in range(TT):
            for c in range(KC):
                m = mm(chain_bank[:, t * NE:(t + 1) * NE], srcT[buf][:, c, t * P:(t + 1) * P], rw[:, c, :],
                       c == 0, c == KC - 1, free["chain"], srcT_ready[bi], all_weights,
                       done=(t == TT - 1 and c == KC - 1))
        srcT_read[buf] = m
        yield True
        rb_all = rb[:].rearrange("p (o n) -> p o n", o=1).to_broadcast((P, TT, NE))
        lg = dve.do(lambda e: e.tensor_tensor(logit[:], chain_bank[:, 0:TT * NE].rearrange(
            "p (t n) -> p t n", t=TT), rb_all, ALU.add), m, all_weights)
        free["chain"] = lg
        yield False
        mx = dve.do(lambda e: e.tensor_reduce(lmax[:], logit[:], AX, ALU.max), lg)
        bc = lambda v: v[:].rearrange("p (t o) -> p t o", o=1).to_broadcast((P, TT, NE))
        sh = dve.do(lambda e: e.tensor_tensor(lwork[:], logit[:], bc(lmax), ALU.subtract), mx)
        ex = act.do(lambda e: e.activation(logit[:], lwork[:], ACT.Exp), sh)
        eq = dve.do(lambda e: e.tensor_scalar(lwork[:], lwork[:], 0.0, None, ALU.is_equal), ex)
        eq = dve.do(lambda e: e.tensor_tensor(lwork[:], lwork[:], first_wins[:], ALU.mult), eq, ready)
        fm = dve.do(lambda e: e.tensor_reduce(lmax[:], lwork[:], AX, ALU.max), eq)
        yield False
        oh = dve.do(lambda e: e.tensor_tensor(lwork[:], lwork[:], bc(lmax), ALU.is_equal), fm)
        sm = dve.do(lambda e: e.tensor_reduce(lsum[:], logit[:], AX, ALU.add), ex)
        sm = dve.do(lambda e: e.reciprocal(lsum[:], lsum[:]), sm)
        gw = dve.do(lambda e: e.tensor_tensor(G[:], lwork[:], bc(lsum), ALU.mult), oh, sm, state["gate_read"][buf])
        state["gate_ready", bi] = gw
        yield False

    def next_bulk():
        state["bulk"] = i = 1 - state.get("bulk", 1)
        return i, bulk_banks[i]

    def experts_job(bi, quarter):
        buf = bi % 2
        for ex in range(2 * quarter, 2 * quarter + 2):
            s = ex % 2
            win = load(w_expert[s][:], a["expert_w"][ex], expert_in[s], state["experts"][s])
            for t in range(0, TT, 2):
                bk_i, bulk = next_bulk()
                for i in range(2):
                    for c in range(KC):
                        m = mm(bulk[:, i * D:(i + 1) * D], srcT[buf][:, c, (t + i) * P:(t + i + 1) * P],
                               w_expert[s][:, c, :], c == 0, c == KC - 1, free[bk_i], win,
                               srcT_ready[bi], done=(i == 1 and c == KC - 1))
                        yield True
                state["experts"][s] = m
                for i in range(2):
                    key = ("moe", bi, t + i)
                    last = dve.do(lambda e, i=i, t=t, ex=ex, bulk=bulk: e.scalar_tensor_tensor(
                        out=acc[buf][:, t + i, :], in0=bulk[:, i * D:(i + 1) * D],
                        scalar=gate_w[buf][:, t + i, ex:ex + 1], in1=acc[buf][:, t + i, :],
                        op0=ALU.mult, op1=ALU.add), m, state["gate_ready", bi], state.get(key))
                    state[key] = last
                free[bk_i] = last
                yield False
        srcT_read[buf] = m
        acc_ready[bi] = last

    def quad_job(n):
        bi, quad = divmod(n, NQ)
        layer, _ = blocks[bi]
        buf, slot = bi % 2, n % 3
        w = w0qk if layer == 0 else w1qk
        q0 = 0 if quad % 2 == 0 else 64
        k0 = 64 - q0
        for half in range(2):
            cols = slice(half * HALF, (half + 1) * HALF)
            for c in range(KC):
                m = mm(chain_bank[:], w[:, c, quad, :], srcT[buf][:, c, cols], c == 0, c == KC - 1,
                       free["chain"], srcT_ready[bi], all_weights, done=(c == KC - 1))
                yield True
            if layer == 0:
                bias = b0qk[:, quad:quad + 1]
                hi = act.do(lambda e, cols=cols, bias=bias: e.activation(
                    part[0][:, cols], chain_bank[:], ACT.Identity, bias=bias), m, state["parts_read"], all_weights)
                r = dve.do(lambda e, cols=cols, bias=bias: e.scalar_tensor_tensor(
                    out=rest[:], in0=chain_bank[:], scalar=bias, in1=part[0][:, cols],
                    op0=ALU.add, op1=ALU.subtract), hi, state["rest_read"])
                free["chain"] = r
            else:
                g = metric[q0:q0 + 64, quad // 2, cols]
                a1 = dve.do(lambda e, g=g: e.tensor_tensor(gated[q0:q0 + 64, :], chain_bank[q0:q0 + 64, :], g,
                                                           ALU.mult), m, metric_ready[bi, quad // 2], state["gated_read"])
                a2 = act.do(lambda e: e.copy(gated[k0:k0 + 64, :], chain_bank[k0:k0 + 64, :]), m, state["gated_read"])
                state["metric_read"][quad // 2] = a1
                pe.wait(a1)
                free["chain"] = a2
                hi = dve.do(lambda e, cols=cols: e.tensor_copy(part[0][:, cols], gated[:]), a1, a2, state["parts_read"])
                r = pool.do(lambda e, cols=cols: e.tensor_tensor(rest[:], gated[:], part[0][:, cols], ALU.subtract),
                            hi, state["rest_read"])
                state["gated_read"] = r
            mid = pool.do(lambda e, cols=cols: e.tensor_scalar(part[1][:, cols], rest[:], 1.0, 0.0, ALU.mult, ALU.add),
                          r, state["parts_read"])
            lo = pool.do(lambda e, cols=cols: e.tensor_tensor(part[2][:, cols], rest[:], part[1][:, cols], ALU.subtract),
                         mid, state["parts_read"])
            state["rest_read"] = lo
            yield False
        srcT_read[buf] = m
        for i, (pq, pk) in enumerate(zip(Q_ORDER, K_ORDER)):
            rows = slice(i * BLK, (i + 1) * BLK)
            load(qstack[slot][rows, :, :], part[pq][q0:q0 + 64, :], stack_in[slot], hi, lo, stack_read[slot])
            mark = load(kstack[slot][rows, :, :], part[pk][k0:k0 + 64, :], stack_in[slot])
        stack_ready[n] = mark
        state["parts_read"] = mark
        yield False

    def metric_job(bi):
        hidden = hid[:].rearrange("p (m n) -> p m n", m=MT)
        for half in range(2):
            cols = slice(half * HALF, (half + 1) * HALF)
            for mt in range(MT):
                bk_i, bulk = next_bulk()
                for c in range(KC):
                    m = mm(bulk[:], wm1[:, c, mt * P:(mt + 1) * P], normT[:, c, cols], c == 0, c == KC - 1,
                           free[bk_i], normT_ready[bi], all_weights, done=(c == KC - 1))
                    yield True
                th = act.do(lambda e, mt=mt, bulk=bulk: e.activation(hidden[:, mt, :], bulk[:], ACT.Tanh,
                                                          bias=bm1[:, mt:mt + 1]), m, state["hid_read"], state["bm1_ready"], *state["butterfly_done"])
                free[bk_i] = th
                yield False
            for pair in range(2):
                bk_i, bulk = next_bulk()
                for kt in range(MT):
                    m = mm(bulk[:], wm2[:, kt, pair, :], hidden[:, kt, :], kt == 0, kt == MT - 1,
                           free[bk_i], th, done=(kt == MT - 1))
                    yield True
                g = metric[:, pair, cols]
                t2 = act.do(lambda e, g=g, pair=pair, bulk=bulk: e.activation(g, bulk[:], ACT.Tanh, bias=bm2[:, pair:pair + 1]),
                            m, state["metric_read"][pair])
                free[bk_i] = t2
                metric_ready[bi, pair] = dve.do(lambda e, g=g, pair=pair: e.tensor_scalar(
                    g, g, 0.1, eta[:, pair:pair + 1], ALU.mult, ALU.add), t2, ready)
                yield False
            state["hid_read"] = m
        state["normT_read"] = m

    def ffn_job(bi, quarters):
        buf = bi % 2
        Q = T // 4
        hidden = hid[:].rearrange("p (h n) -> p h n", h=HT)
        for q in quarters:
            cols = slice(q * Q, (q + 1) * Q)
            for ht in range(0, HT, 2):
                bk_i, bulk = next_bulk()
                for i in range(2):
                    for c in range(KC):
                        m = mm(bulk[:, i * Q:(i + 1) * Q], wexp[:, c, (ht + i) * P:(ht + i + 1) * P],
                               normT[:, c, cols], c == 0, c == KC - 1, free[bk_i], normT_ready[bi],
                               state["ffn_ready"], state["ffn_ready1"], state["ffn_ready2"], done=(i == 1 and c == KC - 1))
                        yield True
                ev = dve.do(lambda e, ht=ht, bulk=bulk: e.tensor_tensor(
                    hidden[:, ht:ht + 2, :], bulk[:].rearrange("p (h n) -> p h n", h=2),
                    bexp[:, ht:ht + 2].rearrange("p (h o) -> p h o", o=1).to_broadcast((P, 2, Q)), ALU.add),
                    m, state["hid_read"], state["ffn_bias"])
                free[bk_i] = ev
                yield False
            state["normT_read"] = m
            ge = act.do(lambda e: e.activation(hid[:], hid[:], ACT.Gelu), ev)
            yield False
            bk_i, bulk = next_bulk()
            for i in range(2):
                for ht in range(HT):
                    m = mm(bulk[:, i * D:(i + 1) * D], hidden[:, ht, i * P:(i + 1) * P], wcon[:, ht, :],
                           ht == 0, False, free[bk_i], ge)
                    yield True
                m = mm(bulk[:, i * D:(i + 1) * D], ones_row[:], bcon[:], False, True, state["bcon_ready"],
                       ready, done=(i == 1))
            state["hid_read"] = m
            yield True
            view = acc[buf][:, 2 * q:2 * q + 2, :]
            last = dve.do(lambda e, view=view, bulk=bulk: e.tensor_tensor(view, bulk[:].rearrange("p (t d) -> p t d", t=2),
                                                               view, ALU.add), m, acc_loaded[bi])
            free[bk_i] = last
            yield False
        acc_ready[bi] = last

    butterfly_in, wcon_in = sem("butterfly_in"), sem("wcon_in")

    def butterfly_job():
        bw_in = butterfly_in
        weights_read = ()
        done = (all_weights, all_weights)
        for stage in range(STAGES):
            win = load(bf_w, a["up"][stage].rearrange("(o c) j -> o c j", o=1).to_broadcast((P, 4, FH // 2)),
                       butterfly_in, *weights_read)
            done = yield from butterfly_stage(stage, ((pool, wexp[:, 0, :]), (dve, wexp[:, 1, :]), (dve, bias_row)),
                                              (0, 1, 2, 3), win, done, weights_read)
            weights_read = done
        state["ffn_ready"], state["ffn_ready1"] = done
        for ht in range(HT):
            m = pe.do(lambda e, ht=ht: e.transpose(chain_bank[:, ht:ht + 1], bias_row[0:1, ht * P:(ht + 1) * P],
                                                   ident[0:1, 0:1]), free["chain"], state["ffn_ready1"],
                      signal=(ht == HT - 1))
        yield True
        state["ffn_bias"] = dve.do(lambda e: e.tensor_tensor(bexp[:], chain_bank[:, 0:HT], upb[:], ALU.add), m, all_weights)
        free["chain"] = state["ffn_bias"]
        state["bcon_ready"] = dve.do(lambda e: e.tensor_tensor(bcon[:], bcon[:], dbias, ALU.add), all_weights)
        wt_in = wcon_in
        held = [normT[:, i, :] for i in range(KC)]
        for i in range(KC):
            dn = load(held[i], a["wconT"][i * P:(i + 1) * P, :], wt_in, m, state["bcon_ready"])
        done = (dn, dn)
        for stage in reversed(range(STAGES)):
            win = load(bf_w, a["down"][stage].rearrange("(o c) j -> o c j", o=1).to_broadcast((P, 4, FH // 2)),
                       butterfly_in, *weights_read)
            done = yield from butterfly_stage(stage, ((pool, held[0]), (dve, held[1])), (0, 2, 1, 3), win, done,
                                              weights_read)
            weights_read = done
        for ht in range(0, HT, 2):
            for i in range(2):
                for tile in range(KC):
                    m = pe.do(lambda e, i=i, tile=tile, ht=ht: e.transpose(
                        chain_bank[:, (i * 2 + tile) * P:(i * 2 + tile + 1) * P],
                        held[tile][:, (ht + i) * P:(ht + i + 1) * P], ident[:]), free["chain"], *done, id_ready,
                        signal=(i == 1 and tile == 1))
            yield True
            last = act.do(lambda e, ht=ht: e.copy(wcon[:, ht:ht + 2, :], chain_bank[:].rearrange("p (h d) -> p h d", h=2)), m)
            free["chain"] = last
            yield False
        state["normT_read"] = m
        state["ffn_ready2"] = last
        state["bm1_ready"] = dve.do(lambda e: e.tensor_tensor(bm1[:], bm1[:], wm1c[:], ALU.subtract), all_weights)
        state["butterfly_done"] = weights_read
        yield False

    def butterfly_stage(stage, tiles, order, win, done, before):
        s = 2 ** stage
        result = {}
        for half in range(2):
            for lane, rows in tiles:
                p = rows.shape[0]
                y = rows.rearrange("p (n a s) -> p n a s", a=2, s=s)
                n, w = y.shape[1], min(s, HALF // 2)
                ns = slice(half * n // 2, (half + 1) * n // 2) if n > 1 else slice(0, 1)
                ss = slice(0, s) if n > 1 else slice(half * w, (half + 1) * w)
                va, vb = y[:, ns, 0, ss], y[:, ns, 1, ss]
                t = bf_t[:, 0:2, :] if lane is pool else bf_t[:, 2:4, :]
                t = t.rearrange("p a b -> p (a b)").rearrange("p (i n s) -> p i n s", i=4, s=w)
                wt = bf_w[:, :, half * HALF // 2:(half + 1) * HALF // 2].rearrange("p i (n s) -> p i n s", s=w)
                ydone = done[0] if lane is pool else done[1]
                for i, src in enumerate((va, vb, va, vb)):
                    m = lane.do(lambda e, i=i, src=src, t=t, wt=wt, p=p: e.tensor_tensor(
                        t[0:p, i], src, wt[0:p, order[i]], ALU.mult), win, ydone, result.get(lane.name), *before)
                lane.do(lambda e, t=t, va=va, p=p: e.tensor_tensor(va, t[0:p, 0], t[0:p, 1], ALU.add), m)
                result[lane.name] = lane.do(lambda e, t=t, vb=vb, p=p: e.tensor_tensor(
                    vb, t[0:p, 2], t[0:p, 3], ALU.add), m)
                yield False
        return result["pool"], result["dve"]

    def load_job(bi):
        layer, b = blocks[bi]
        buf = bi % 2
        src = x_dram[b] if layer == 0 else x1_dram[b]
        acc_loaded[bi] = load(acc[buf][:], src, x_in[buf], state.get(("stored", buf)),
                              state["x1"].get(b) if layer == 1 else None)
        yield False

    def finish_job(bi):
        layer, b = blocks[bi]
        buf = bi % 2
        O = tok[buf]
        w = w0o if layer == 0 else w1o
        for t in range(0, TT, 2):
            if layer == 0 and t % 4 == 0:
                for i in range(4):
                    m = pe.do(lambda e, i=i, t=t: e.transpose(
                        chain_bank[0:NE, i * P:(i + 1) * P], gate_w[buf][:, t + i, :], ident[:]),
                        free["chain"], state["gate_ready", bi], id_ready, signal=(i == 3))
                state["gate_read"][buf] = m
                yield True
                gates = dve.do(lambda e: e.tensor_copy(gateT[:], chain_bank[0:NE, :]), m, state["gateT_read"])
                free["chain"] = gates
                yield False
            for i in range(4):
                m = pe.do(lambda e, i=i, t=t: e.transpose(
                    chain_bank[:, i * P:(i + 1) * P], O[:, t + i // 2, (i % 2) * P:(i % 2 + 1) * P], ident[:]),
                    free["chain"], heads_out[bi], signal=(i == 3))
            tok_read[buf] = m
            yield True
            ev = act.do(lambda e: e.copy(turned[:], chain_bank[:]), m, state["turned_read"])
            free["chain"] = ev
            yield True
            for i in range(2):
                for c in range(KC):
                    last = layer == 1 and c == KC - 1
                    m = mm(chain_bank[:, i * D:(i + 1) * D], turned[:, (2 * i + c) * P:(2 * i + c + 1) * P], w[:, c, :],
                           c == 0, last, ev, free["chain"], done=(last and i == 1))
                    yield True
                if layer == 0:
                    mm(chain_bank[:, i * D:(i + 1) * D], ones_row[:], b0o[:], False, False, ready)
                    m = mm(chain_bank[:, i * D:(i + 1) * D], gateT[:, (t % 4 + i) * P:(t % 4 + i + 1) * P], expert_b[:],
                           False, True, gates, done=(i == 1))
            state["turned_read"] = m
            if layer == 0:
                state["gateT_read"] = m
            yield True
            view = acc[buf][:, t:t + 2, :]
            pv = chain_bank[:].rearrange("p (t d) -> p t d", t=2)
            if layer == 0:
                last = dve.do(lambda e, view=view, pv=pv: e.tensor_tensor(view, pv, view, ALU.add), m, acc_ready[bi])
                free["chain"] = last
            else:
                g2 = gated[:].rearrange("p (t d) -> p t d", t=2)
                z = dve.do(lambda e: e.tensor_scalar(gated[:], chain_bank[:], 0.1, 8.0, ALU.mult, ALU.min), m, state["gated_read"])
                free["chain"] = z
                z = dve.do(lambda e: e.tensor_scalar(gated[:], gated[:], -8.0, None, ALU.max), z)
                for i in range(2):
                    sq = dve.do(lambda e, i=i: e.scalar_tensor_tensor(
                        out=rest[:, 0:D - 1], in0=g2[:, i, 1:D], scalar=1.0, in1=g2[:, i, 1:D], op0=ALU.mult,
                        op1=ALU.mult, accum_out=zsum[:, i:i + 1]), z, state["rest_read"])
                    state["rest_read"] = sq
                sq = dve.do(lambda e: e.tensor_scalar(zsum[:], zsum[:], 1.0, EPS, ALU.add, ALU.add), sq)
                x0 = pool.do(lambda e: e.tensor_tensor(g2[:, :, 0:1], zsum[:].rearrange("p (t o) -> p t o", o=1),
                                                       power[:, 1, 0:2].rearrange("p (t o) -> p t o", o=1), ALU.pow), sq, z)
                yield True
                last = dve.do(lambda e, view=view, g2=g2: e.tensor_tensor(view, g2, view, ALU.add), x0, acc_ready[bi])
                state["gated_read"] = last
            dst = x1_dram[b] if layer == 0 else out_dram[b]
            store = sp.do(lambda e, view=view, dst=dst, t=t: e.dma_start(dst[:, t:t + 2, :], view), last,
                          done=acc_out[buf], by=16)
            yield False
        state[("stored", buf)] = store
        if layer == 0:
            state["x1"][b] = store

    zsum = sb("zsum", [P, 2])

    def heads_job(n, hq):
        bi, quad = divmod(n, NQ)
        O = tok[bi % 2]
        yield False, state["headsT"]
        for i in range(4):
            m = pe.do(lambda e, i=i: e.transpose(chain_bank[:, i * P:(i + 1) * P], headsT[:, i * P:(i + 1) * P], ident[:]),
                      free["chain"], state["headsT"], signal=(i == 3))
        state["headsT_read"] = m
        state["heads_taken"] = True
        yield True
        bk = chain_bank[:].rearrange("p (t h r) -> p t h r", t=4, h=QH)
        rc = dve.do(lambda e: e.reciprocal(recip[:].rearrange("p t (h o) -> p t h o", o=1), bk[:, :, :, HS:HS + 1]),
                    m, state["recip"])
        dst = O[:, hq * 4:hq * 4 + 4, quad * 64:(quad + 1) * 64].rearrange("p t (h d) -> p t h d", h=QH)
        last = dve.do(lambda e: e.tensor_tensor(dst, bk[:, :, :, 0:HS], recip[:].rearrange(
            "p t (h o) -> p t h o", o=1).to_broadcast((P, 4, QH, HS)), ALU.mult), rc, tok_read[bi % 2])
        state["recip"] = last
        free["chain"] = last
        heads_out[bi] = last
        yield False

    def maxes_job(n):
        slot, mb = n % 3, n % 2
        M = maxes[mb]
        m = dve.do(lambda e: e.tensor_tensor(negmax[:].rearrange("p (h t) -> p h t", h=QH), M[:, 0, :, :],
                                             M[:, 1, :, :], ALU.min), (dve_max, dve_max.n), state.get("negmax_read"))
        maxes_read[mb] = m
        yield False
        m = pe.do(lambda e: e.transpose(chain_bank[0:QH * TT, 0:P], negmax[:], ident[:]), m, free["chain"])
        state["negmax_read"] = m
        yield True
        mp = mpart[mb]
        src = chain_bank[0:QH * TT, 0:P]
        h = dve.do(lambda e: e.tensor_copy(mp[:, 0, :], src), m, state["mpart"])
        r = dve.do(lambda e: e.tensor_tensor(mrest[:], src, mp[:, 0, :], ALU.subtract), h)
        free["chain"] = r
        md = dve.do(lambda e: e.tensor_copy(mp[:, 1, :], mrest[:]), r)
        lo = dve.do(lambda e: e.tensor_tensor(mp[:, 2, :], mrest[:], mp[:, 1, :], ALU.subtract), md)
        for i in range(3):
            mark = load(qstack[slot][SROWS + i:SROWS + i + 1, :, :], mp[:, i, :], stackm_in[slot], lo, stack_read[slot])
        stackm_ready[n] = mark
        state["mpart"] = mark
        yield False

    def first_pass(n):
        bi, _ = divmod(n, NQ)
        layer, _ = blocks[bi]
        slot, M = n % 3, maxes[n % 2]
        pe.wait(k_ones)
        if layer == 0:
            dve.do(lambda e: e.memset(M[:, 1, :, 0:4], BIG), maxes_read[n % 2], done=dve_max)
        for j in range(QH):
            for t in range(TT):
                for half in range(2):
                    width = HALF
                    if layer == 0:
                        width = min(HALF, (t + 1) * P - half * HALF)
                        if width <= 0:
                            continue
                    i = first_pass.count % 2
                    first_pass.count += 1
                    bk = max_bank[i]
                    diag = layer == 0 and half == t // 4
                    m = mm(bk[:, 0:width], qstack[slot][0:SROWS, j, t * P:(t + 1) * P],
                           kstack[slot][0:SROWS, j, half * HALF:half * HALF + width], True, not diag,
                           stack_ready[n], max_free[i], done=not diag, counter=pe_max)
                    if diag:
                        m = mm(bk[:, width - P:width], ident_bf[:], causal[:], False, True, causal_ready,
                               done=True, counter=pe_max)
                    max_free[i] = dve.do(lambda e, bk=bk, width=width, half=half, j=j, t=t: e.tensor_reduce(
                        M[:, half, j, t:t + 1], bk[:, 0:width], AX, ALU.max, negate=True), m, maxes_read[n % 2],
                        done=dve_max, price=65 + width / 0.96)
                    yield
    first_pass.count = 0

    def second_pass(n):
        bi, quad = divmod(n, NQ)
        layer, _ = blocks[bi]
        slot = n % 3
        for hq in range(2):
            nk = TT if layer == 1 or hq == 1 else 4
            for kt in range(nk):
                c0 = max(0, kt * P - hq * HALF) if layer == 0 else 0
                pb = second_pass.count % 2
                second_pass.count += 1
                for j in range(QH):
                    i = j % 2
                    score_next[0] = 1 - i
                    m = mm(score_bank[i][:, c0:HALF], kstack[slot][0:SROWS + MROWS, j, kt * P:(kt + 1) * P],
                           qstack[slot][0:SROWS + MROWS, j, hq * HALF + c0:(hq + 1) * HALF], True, True,
                           score_free[i], stack_ready[n], stackm_ready[n], done=True, counter=pe_scores)
                    e_ = act.do(lambda e, i=i, j=j, c0=c0, pb=pb: e.activation(prob[pb][:, j, c0:HALF],
                                score_bank[i][:, c0:HALF], ACT.Exp, scale=SCALE), m, second_pass.read[pb], done=act_exp,
                                price=50 + (HALF - c0) / 1.2)
                    score_free[i] = e_
                    if j == 2 and second_pass.pending:
                        yield None
                        yield product(*second_pass.pending)
                    elif j < QH - 1:
                        yield None
                masked = e_
                if layer == 0 and kt * P >= hq * HALF:
                    view = prob[pb][:, :, c0:c0 + P]
                    masked = pool.do(lambda e, view=view: e.affine_select(
                        out=view, in_=view, compare_op=ALU.is_ge, fill=0.0, base=0,
                        pattern=[[0, QH], [1, P]], channel_multiplier=-1), e_)
                second_pass.pending = (n, hq, kt, nk, c0, pb, masked)
                yield None
        stack_read[slot] = (pe_scores, pe_scores.n)

    def product(n, hq, kt, nk, c0, pb, masked):
        bi, quad = divmod(n, NQ)
        V = values[bi % 2]
        for j in range(QH):
            m = pe.do(lambda e, j=j: e.matmul(pv_bank[32 * j:32 * j + VC, c0:HALF], V[:, kt, QH * quad + j, :],
                                              prob[pb][:, j, c0:HALF], start=(kt == 0), stop=(kt == nk - 1)),
                      masked, values_ready[bi], free["pv"] if kt == 0 else None, signal=(j == QH - 1), price=(HALF - c0) * 1.05 / 2.4)
        second_pass.read[pb] = values_read[bi % 2] = m
        second_pass.pending = None
        if kt < nk - 1:
            return None
        assert state.get("heads_taken", True)
        state["heads_taken"] = False
        state["headsT"] = free["pv"] = act.do(lambda e: e.copy(headsT[:], pv_bank[:]), m, state.get("headsT_read"))
        return n, hq
    second_pass.count, second_pass.read, second_pass.pending = 0, [None, None], None

    class Stream:

        def __init__(self):
            self.jobs, self.urgent, self.held, self.now, self.wake = [], [], False, None, 0.0

        def step(self):
            if self.now is None or (not self.held and self.urgent and not self.now[1]):
                if self.urgent:
                    if self.now is not None:
                        self.jobs.insert(0, self.now[0])
                    self.now = (self.urgent.pop(0), True)
                elif self.jobs:
                    self.now = (self.jobs.pop(0), False)
                else:
                    return False
            try:
                self.held = next(self.now[0])
                self.wake = Lane.wake
                if isinstance(self.held, tuple):
                    self.held, self.wake = self.held[0], when(self.held[1])
            except StopIteration:
                self.now, self.held = None, False
            return True

        def hurry(self):
            return (self.now[1] if self.now else False) or (bool(self.urgent) and not self.held)

        def empty(self):
            return self.now is None and not self.jobs and not self.urgent

        def drain(self):
            while not self.empty():
                self.step()

    chain, bulk = Stream(), Stream()
    butter_credit = [0.0]
    score_next = [0]

    def jobs_of(period):
        bi, q = divmod(period, NQ)
        cj, bj = [], []
        if period + 2 < NP_:
            cj.append(quad_job(period + 2))
        nb = bi + 1
        two_in_a_row = nb < NBL and blocks[bi][0] == 1 and blocks[nb][0] == 1
        if q == two_in_a_row and nb < NBL:
            cj.append(norm_job(nb))
        if q == 1 and nb < NBL:
            cj.append(values_job(nb))
            if blocks[nb][0] == 0:
                cj.append(router_job(nb))
        if q in (2, 3) and nb < NBL:
            bj.append(ffn_job(nb, (q - 2,)) if blocks[nb][0] == 1 else experts_job(nb, q - 2))
        if q == 0:
            bj.append(ffn_job(bi, (2, 3) if two_in_a_row else (2,)) if blocks[bi][0] == 1 else experts_job(bi, 2))
        if q == 1 and not two_in_a_row:
            bj.append(ffn_job(bi, (3,)) if blocks[bi][0] == 1 else experts_job(bi, 3))
        if q == 1 and nb < NBL and blocks[nb][0] == 1 and not two_in_a_row:
            bj.append(metric_job(nb))
        return cj, bj, two_in_a_row

    def run_all(*jobs):
        for g in jobs:
            for _ in g:
                pass

    run_all(norm_job(0), values_job(0), router_job(0), quad_job(0), quad_job(1), load_job(1), first_pass(0),
            maxes_job(0))

    butter = [butterfly_job()]
    did = {}
    bulk.jobs += [experts_job(0, 0), experts_job(0, 1)]
    for period in range(NP_):
        bi, q = divmod(period, NQ)
        cj, bj, two_in_a_row = jobs_of(period)
        chain.jobs += cj
        bulk.jobs += bj
        atten = second_pass(period)
        first = first_pass(period + 1) if period + 1 < NP_ else iter(())

        def step_second():
            ev = next(atten, "end")
            if ev == "end":
                return False
            if ev is not None:
                chain.urgent.append(heads_job(*ev))
                n, hq = ev
                if hq == 1 and n % NQ == NQ - 1:
                    chain.jobs.insert(0, finish_job(n // NQ))
                    if n // NQ + 2 < NBL:
                        chain.jobs.insert(1, load_job(n // NQ + 2))
            return True

        def step_first():
            if next(first, "end") == "end":
                if period + 1 < NP_:
                    chain.urgent.append(maxes_job(period + 1))
                return False
            return True

        def step_butterfly():
            if not butter or chain.held:
                return bool(butter)
            held = next(butter[0], "end")
            while held is True:
                held = next(butter[0], "end")
            if held == "end":
                butter.clear()
                return False
            return True

        steps = {"second": step_second, "first": step_first, "chain": chain.step, "bulk": bulk.step}
        ahead = {"second": 1.0, "first": FIRST_AHEAD, "chain": 1.1, "bulk": 1.0}
        live, work = dict(steps), dict.fromkeys(steps, 0.0)
        def ready_at(s):
            if s == "second":
                return when(score_free[score_next[0]])
            if s == "first":
                return when(max_free[first_pass.count % 2])
            return (chain if s == "chain" else bulk).wake

        while live:
            def progress(s):
                return work[s] / plan.get((period, s), 1.0) / ahead[s]
            startable = [s for s in live if ready_at(s) <= pe.clock + SLACK]
            s = min(startable, key=progress) if startable else min(live, key=ready_at)
            if "second" in live and s != "chain" and chain.hurry() and chain.wake <= pe.clock + SLACK:
                s = "chain"
            before = Lane.cost
            fn = steps[s]
            if not fn():
                if s in live:
                    del live[s]
            work[s] += max(Lane.cost - before, 1.0)
            if period <= NQ and butter:
                butter_credit[0] += BUTTER_RATE
                while butter_credit[0] > 1 and step_butterfly():
                    butter_credit[0] -= 1
        for s in steps:
            did[period, s] = work[s]
        chain.drain()
        bulk.drain()
        if period == NQ - 1 and butter:
            while chain.held:
                chain.step()
            run_all(butter.pop())
        if q == 1 and two_in_a_row:
            run_all(metric_job(bi + 1))
    run_all(heads_job(*product(*second_pass.pending)), finish_job(NBL - 1))
    for c in acc_out:
        sp.wait((c, c.n))
    return did, (sp, pe, act, dve, pool)


def build(nc, aps, out):
    with ExitStack() as ctx:
        mem = Memory(nc, ctx)
        plan, _ = two_layers(mem, aps, out, {})
        plan, _ = two_layers(mem, aps, out, plan)
        _, (sp, pe, act, dve, pool) = two_layers(mem, aps, out, plan)
        with nc.Block() as block:
            block.sync(sp.run)
            block.tensor(pe.run)
            block.scalar(act.run)
            block.vector(dve.run)
            block.gpsimd(pool.run)


def kernel(**inputs):
    import concourse.bacc as bacc
    from concourse.bass_utils import run_bass_kernel_spmd

    g = {k: np.asarray(v) for k, v in inputs.items()}

    def rows(w):
        return w.reshape(w.shape[0] // P, P, -1).transpose(1, 0, 2)

    def quad_cols(w):
        w = w.reshape(*w.shape[:-1], NQ, QH, HS)
        return np.swapaxes(w, -1, -2).reshape(*w.shape[:-3], NQ, QH * HS)

    def qk_cols(q, k):
        q, k = quad_cols(q), quad_cols(k)
        even = np.concatenate([q, k], -1)
        odd = np.concatenate([k, q], -1)
        pick = [even[..., i, :] if i % 2 == 0 else odd[..., i, :] for i in range(NQ)]
        return np.stack(pick, -2)

    w0 = g["L0_attn_attn_W"].reshape(D, H, 3, HS)
    b0 = g["L0_attn_attn_b"].reshape(H, 3, HS)
    flat = lambda w: w.reshape(*w.shape[:-2], H * HS)
    w2q = quad_cols(g["L1_attn_W2"].T)
    b2q = quad_cols(g["L1_attn_b2"])
    host = {
        "x": g["L0_attn_encodings"],
        "w0qk": rows(qk_cols(flat(w0[:, :, 0]), flat(w0[:, :, 1])).reshape(D, NQ * P)).reshape(P, KC, NQ, P),
        "b0qk": qk_cols(flat(b0[:, 0]), flat(b0[:, 1])).T,
        "w0v": rows(flat(w0[:, :, 2])),
        "b0v": flat(b0[:, 2]),
        "w0o": rows(g["L0_attn_out_W"]),
        "b0o": g["L0_attn_out_b"][None, :],
        "rw": rows(g["L0_ffn_router_w"]),
        "rb": g["L0_ffn_router_b"],
        "expert_w": g["L0_ffn_expert_w"].reshape(NE, KC, P, D).transpose(0, 2, 1, 3),
        "expert_b": g["L0_ffn_expert_b"],
        "w1qk": rows(qk_cols(g["L1_attn_Wq"].T, g["L1_attn_Wk"].T).reshape(D, NQ * P)).reshape(P, KC, NQ, P),
        "w1v": rows(g["L1_attn_Wv"].T),
        "w1o": rows(g["L1_attn_Wo"].T),
        "wm1": rows(g["L1_attn_W1"].T),
        "bm1": g["L1_attn_b1"].reshape(MT, P).T,
        "wm1c": g["L1_attn_W1"][:, 0].reshape(MT, P).T,
        "wm2": w2q.reshape(MT, P, 2, P).transpose(1, 0, 2, 3),
        "bm2": b2q.reshape(2, P).T,
        "wexp": rows(g["L1_ffn_W_exp"]),
        "b_exp": g["L1_ffn_b_exp"][None, :],
        "upb": g["L1_ffn_up_bias"].reshape(HT, P).T,
        "up": g["L1_ffn_up_weights"].reshape(STAGES, FH // 2, 4).transpose(0, 2, 1),
        "down": g["L1_ffn_down_weights"].reshape(STAGES, FH // 2, 4).transpose(0, 2, 1),
        "wconT": g["L1_ffn_W_con"].T,
        "b_con": g["L1_ffn_b_con"][None, :],
        "down_bias": g["L1_ffn_down_bias"][None, :],
    }
    nc = bacc.Bacc("TRN2", target_bir_lowering=False, num_devices=1, dynamic_dma_scratch_size=1024)
    arrays, aps = {}, {}
    for name, v in host.items():
        v = np.ascontiguousarray(v)
        arrays["in_" + name] = v
        aps[name] = nc.dram_tensor("in_" + name, v.shape, mybir.dt.from_np(v.dtype), kind="ExternalInput").ap()
    out = nc.dram_tensor("out", (NB, T, D), F32, kind="ExternalOutput").ap()
    build(nc, aps, out)
    r = run_bass_kernel_spmd(nc, [arrays], core_ids=[0])
    return r.results[0]["out"]
```

```python
from contextlib import ExitStack

import numpy as np

import concourse.bass as bass
from concourse import mybir

F32 = mybir.dt.float32
BF16 = mybir.dt.bfloat16
ALU = mybir.AluOpType
ACT = mybir.ActivationFunctionType
AX = mybir.AxisListType.X

P = 128
NB, T, D = 8, 1024, 256
H, HS = 16, 16
QH = 4
NQ = H // QH
TT = T // P
KC = D // P
NE = 8
FH = 1024
HT = FH // P
MH = 2 * D
MT = MH // P
STAGES = 10
HALF = 512
BLK = HS
Q_ORDER = (0, 0, 1, 0, 2, 1)
K_ORDER = (0, 1, 0, 2, 0, 1)
SROWS = BLK * len(Q_ORDER)
MROWS = 3
SCALE = HS ** -0.5
NEG = -1.0e30
BIG = 3.0e38
VC = HS + 1
LN_EPS = 1e-5
EPS = 1e-6
PACE = {"act": 0.8, "dve": 1.0, "pool": 0.6}
FIRST_AHEAD, CHAIN_AHEAD, CHAIN_EARLY = 1.4, 1.1, 2.0
SLACK = 50.0
BUTTER_RATE = 0.5
POW, TINY, POOL_PASS, DVE_PASS, TABLE, BIG_LOAD = 1600, 90, 1100, 600, 1280, 5500
TRANSPOSE, PE_REACH, REACH = 110, 190, 150
INFINITE = 1e18


class Counter:

    def __init__(self, sem):
        self.sem, self.n, self.when = sem, 0, {}

    def add(self, by, when):
        self.n += by
        self.when[self.n] = when
        return self, self.n


class Lane:
    cost = 0.0
    wake = 0.0

    def __init__(self, name, counter, price, reach):
        self.name, self.counter, self.queue, self.known = name, counter, [], {}
        self.price, self.reach, self.clock = price, reach, 0.0

    def wait(self, *marks):
        for m in marks:
            if m is None:
                continue
            counter, value = m
            if self.known.get(id(counter), 0) < value:
                self.known[id(counter)] = value
                self.clock = max(self.clock, counter.when[value])
                self.queue.append(lambda eng, s=counter.sem, v=value: eng.wait_ge(s, v))

    def do(self, fn, *marks, done=None, by=1, signal=True, price=None, lag=0.0):
        self.wait(*marks)
        price = self.price if price is None else price
        Lane.cost += price * PACE.get(self.name, 1.0)
        self.clock += price if self.name != "sp" else 60
        Lane.wake = self.clock + self.reach + lag
        if not signal:
            self.queue.append(lambda eng: fn(eng))
            Lane.wake = 0.0
            return None
        counter = done or self.counter
        mark = counter.add(by, Lane.wake)
        self.queue.append(lambda eng, s=counter.sem: fn(eng).then_inc(s, by))
        return mark

    def run(self, eng):
        for step in self.queue:
            step(eng)


def when(mark):
    return mark[0].when[mark[1]] if mark else 0.0


class Memory:

    def __init__(self, nc, ctx):
        self.nc, self.ctx, self.held = nc, ctx, {}

    def get(self, name, make):
        if name not in self.held:
            self.held[name] = make()
        return self.held[name]


def two_layers(mem, a, out, plan):
    nc, ctx = mem.nc, mem.ctx

    def sb(name, shape, dt=F32):
        return mem.get(name, lambda: ctx.enter_context(nc.sbuf_tensor(name, shape, dt)))

    def bank(name):
        return mem.get(name, lambda: ctx.enter_context(nc.psum_tensor(name, [P, HALF], F32)))

    def sem(name):
        return Counter(mem.get(name, lambda: ctx.enter_context(nc.semaphore(name))))

    pe = Lane("pe", sem("pe_done"), TRANSPOSE, PE_REACH)
    act = Lane("act", sem("act_done"), 480, REACH)
    dve = Lane("dve", sem("dve_done"), 350, REACH)
    pool = Lane("pool", sem("pool_done"), 600, REACH)
    sp = Lane("sp", None, 60, 2500)
    pe_scores, pe_max = sem("pe_scores"), sem("pe_max")
    act_exp, dve_max = sem("act_exp"), sem("dve_max")
    weights_in = sem("weights_in")

    def load(dst, src, counter, *marks, lag=0.0):
        return sp.do(lambda e: e.dma_start(dst, src), *marks, done=counter, by=16, lag=lag)

    max_bank = [bank("max0"), bank("max1")]
    score_bank = [bank("score0"), bank("score1")]
    pv_bank = bank("pv")
    chain_bank = bank("chain")
    bulk_banks = [bank("bulk0"), bank("bulk1")]
    max_free, score_free = [None, None], [None, None]
    free = {"chain": None, 0: None, 1: None, "pv": None}

    ident, ident_bf = sb("ident", [P, P]), sb("ident_bf", [P, P], BF16)
    causal = sb("causal", [P, P], BF16)
    power = sb("power", [P, 2, TT])
    w0qk, b0qk = sb("w0qk", [P, KC, NQ, P]), sb("b0qk", [P, NQ])
    w0v, b0v = sb("w0v", [P, KC, D]), sb("b0v", [P, D])
    w0o = sb("w0o", [P, KC, D])
    rw, rb = sb("rw", [P, KC, NE]), sb("rb", [P, NE])
    expert_b = sb("expert_b", [NE + 1, D])
    first_wins = sb("first_wins", [P, TT, NE])
    w1qk, w1v, w1o = sb("w1qk", [P, KC, NQ, P]), sb("w1v", [P, KC, D]), sb("w1o", [P, KC, D])
    wm1, bm1, wm1c = sb("wm1", [P, KC, MH]), sb("bm1", [P, MT]), sb("wm1c", [P, MT])
    wm2, bm2, eta = sb("wm2", [P, MT, 2, P]), sb("bm2", [P, 2]), sb("eta", [P, 2])
    wexp, bexp = sb("wexp", [P, KC, FH]), sb("bexp", [P, HT])
    upb = sb("upb", [P, HT])
    wcon = sb("wcon", [P, HT, D])
    bcon = sb("bcon", [P, D])
    w_expert = [sb(f"w_expert{i}", [P, KC, D]) for i in range(2)]

    qstack = [sb(f"qstack{i}", [P, QH, T], BF16) for i in range(3)]
    kstack = [sb(f"kstack{i}", [P, QH, T], BF16) for i in range(3)]
    values = [sb(f"values{i}", [P, TT, H, VC]) for i in range(2)]
    prob = [sb(f"prob{i}", [P, QH, HALF]) for i in range(2)]
    srcT = [sb(f"srcT{i}", [P, KC, T]) for i in range(2)]
    normT = sb("normT", [P, KC, T])
    acc = [sb(f"acc{i}", [P, TT, D]) for i in range(2)]
    tok = [sb(f"tok{i}", [P, TT, D]) for i in range(2)]
    part = [sb(f"part{i}", [P, T], BF16) for i in range(3)]
    rest, gated = sb("rest", [P, HALF]), sb("gated", [P, HALF])
    hid = sb("hid", [P, 4 * HALF])
    metric = sb("metric", [P, 2, T])
    turned, headsT = sb("turned", [P, HALF]), sb("headsT", [P, HALF])
    maxes = [sb(f"maxes{i}", [P, 2, QH, TT]) for i in range(2)]
    negmax = sb("negmax", [P, QH * TT])
    mrest = sb("mrest", [QH * TT, P])
    mpart = [sb("mpart", [QH * TT, 3, P], BF16)] * 2
    stats, mv = sb("stats", [P, TT, 6]), sb("mv", [P, TT, 2])
    small = sb("small", [P, 12, TT])
    rstd = sb("rstd", [P, TT])
    recip = sb("recip", [P, 4, QH])
    logit = sb("logit", [P, TT, NE])
    lwork = sb("lwork", [P, TT, NE])
    lmax, lsum = sb("lmax", [P, TT]), sb("lsum", [P, TT])
    gate_w = [sb(f"gate_w{i}", [P, TT, NE]) for i in range(2)]
    gateT = sb("gateT", [NE + 1, HALF])
    x1_dram = mem.get("x1", lambda: nc.dram_tensor("x1_scratch", [NB, P, TT, D], F32, kind="Internal").ap())
    bf_w = [metric[:, :, :].rearrange("p a b -> p (a b)").rearrange("p (c j) -> p c j", c=4),
            wcon[:, :, :].rearrange("p a b -> p (a b)").rearrange("p (c j) -> p c j", c=4)]
    bf_t = hid[:, :].rearrange("p (c j) -> p c j", c=4)
    bias_row, dbias = normT[0:1, 0, :], normT[:, 1, 0:D]

    def bcast(ap, n, p=P):
        return ap.rearrange("(o n) -> o n", o=1).to_broadcast((p, n))

    W = {}

    def weight(name, dst, src):
        W[name] = load(dst, src, weights_in)

    x_in = [sem("x_in0"), sem("x_in1")]
    acc_out = [sem("acc_out0"), sem("acc_out1")]
    x_dram = a["x"].rearrange("b (t p) d -> b p t d", p=P, t=TT)
    out_dram = out.rearrange("b (t p) d -> b p t d", p=P, t=TT)
    acc_loaded = {}
    acc_loaded[0] = load(acc[0][:], x_dram[0], x_in[0])
    weight("qk0", w0qk[:], a["w0qk"])
    weight("v0", w0v[:], a["w0v"])
    weight("rw", rw[:], a["rw"])
    weight("b0qk", b0qk[:], a["b0qk"])
    weight("b0v", b0v[:], bcast(a["b0v"], D))
    weight("rb", rb[:], bcast(a["rb"], NE))
    weight("o0", w0o[:], a["w0o"])
    weight("b0o", expert_b[NE:NE + 1, :], a["b0o"])
    weight("eb", expert_b[0:NE, :], a["expert_b"])
    weight("wexp", wexp[:], a["wexp"])
    weight("bexp", bias_row, a["b_exp"])
    weight("upb", upb[:], a["upb"])
    weight("bcon", bcon[:], bcast(a["b_con"], D))
    weight("dbias", dbias, bcast(a["down_bias"], D))
    weight("qk1", w1qk[:], a["w1qk"])
    weight("v1", w1v[:], a["w1v"])
    weight("o1", w1o[:], a["w1o"])
    weight("m1", wm1[:], a["wm1"])
    weight("bm1", bm1[:], a["bm1"])
    weight("m1c", wm1c[:], a["wm1c"])
    weight("m2", wm2[:], a["wm2"])
    weight("bm2", bm2[:], a["bm2"])
    all_weights = (weights_in, weights_in.n)

    zeroed = pool.do(lambda e: e.memset(ident[:], 0.0))
    id_ready = pool.do(lambda e: e.affine_select(out=ident[:], in_=ident[:], compare_op=ALU.not_equal,
                                                 fill=1.0, base=0, pattern=[[-1, P]],
                                                 channel_multiplier=1), zeroed)
    zeroed = pool.do(lambda e: e.memset(ident_bf[:], 0.0))
    idb_ready = pool.do(lambda e: e.affine_select(out=ident_bf[:], in_=ident_bf[:], compare_op=ALU.not_equal,
                                                  fill=1.0, base=0, pattern=[[-1, P]],
                                                  channel_multiplier=1), zeroed)
    zeroed = pool.do(lambda e: e.memset(causal[:], 0.0))
    causal_ready = pool.do(lambda e: e.affine_select(out=causal[:], in_=causal[:], compare_op=ALU.is_ge,
                                                     fill=NEG, base=0, pattern=[[-1, P]],
                                                     channel_multiplier=1), zeroed)
    consts = []
    gate_ones = pool.do(lambda e: e.memset(gateT[:], 1.0))
    pool.wait(gate_ones)
    consts.append(pool.do(lambda e: e.memset(power[:, 0, :], -0.5)))
    consts.append(pool.do(lambda e: e.memset(power[:, 1, :], 0.5)))
    for n in range(NE):
        consts.append(pool.do(lambda e, n=n: e.memset(first_wins[:, :, n:n + 1], float(NE - n))))
    consts.append(dve.do(lambda e: e.memset(eta[:], 1.0)))
    dve.do(lambda e: e.memset(eta[0:1, 0:1], -1.0), consts[-1])
    for i in range(2):
        consts.append(pool.do(lambda e, i=i: e.memset(values[i][:, :, :, HS:VC], 1.0)))
    ready = consts[-1]
    free["pv"] = dve.do(lambda e: e.memset(pv_bank[:], 0.0))

    blocks = [(0, 0), (0, 1)]
    for b in range(NB - 2):
        blocks += [(1, b), (0, b + 2)]
    blocks += [(1, NB - 2), (1, NB - 1)]
    NBL = len(blocks)
    NP_ = NBL * NQ

    srcT_ready, values_ready, normT_ready, metric_ready = {}, {}, {}, {}
    srcT_read, values_read = [None, None], [None, None]
    tok_read, acc_ready = [None, None], {}
    stack_in, stackm_in = [sem(f"stack_in{i}") for i in range(3)], [sem(f"stackm_in{i}") for i in range(3)]
    stack_ready, stackm_ready, stack_read = {}, {}, [None, None, None]
    maxes_read = [None, None]
    state = {"parts_read": None, "rest_read": None, "gated_read": None, "turned_read": None,
             "mpart": None, "hid_read": None, "normT_read": None, "metric_read": [None, None],
             "x1": {}, "ffn": None, "experts": [None, None], "gateT_read": gate_ones,
             "gate_read": [None, None], "recip": None,}
    expert_in = [sem("expert_in0"), sem("expert_in1")]
    heads_out = {}

    def mm(bk, lhsT, rhs, start, stop, *marks, done=False, counter=None):
        n = 1
        for size in rhs.shape[1:]:
            n *= size
        return pe.do(lambda e: e.matmul(bk, lhsT, rhs, start=start, stop=stop), *marks,
                     signal=done, done=counter, price=n * (4 if rhs.dtype == F32 else 1) / 2.4)

    def transpose_block(src, src_ready, dst, dst_free):
        last = None
        for t in range(0, TT, 2):
            for i in range(4):
                tile, c = t + i // 2, i % 2
                marks = (free["chain"], src_ready, id_ready, ready) if i == 0 else ()
                m = pe.do(lambda e, i=i, tile=tile, c=c: e.transpose(
                    chain_bank[:, i * P:(i + 1) * P], src[:, tile, c * P:(c + 1) * P], ident[:]),
                    *marks, signal=(i == 3))
            yield True
            view = dst[:, :, t * P:(t + 2) * P].rearrange("p c (t n) -> p t c n", t=2)
            last = act.do(lambda e, view=view: e.copy(view, chain_bank[:].rearrange(
                "p (t c n) -> p t c n", t=2, c=2)), m, *dst_free)
            free["chain"] = last
            yield False
        return last

    def norm_job(bi):
        layer, b = blocks[bi]
        buf = bi % 2
        x, y = acc[buf], tok[buf]
        xin = acc_loaded[bi]
        for t in range(TT):
            m = dve.do(lambda e, t=t: e.bn_stats(stats[:, t, :], x[:, t, :]), xin)
            if t % 2 == 1:
                yield False
        for t in range(TT):
            m2 = dve.do(lambda e, t=t: e.bn_aggr(mv[:, t, :], stats[:, t, :]), m, price=TINY)
        m2 = dve.do(lambda e: e.tensor_scalar(rstd[:], mv[:, :, 1:2].rearrange("p t o -> p (t o)"),
                                              LN_EPS, None, ALU.add), m2, price=TINY)
        r = pool.do(lambda e: e.tensor_tensor(rstd[:], rstd[:], power[:, 0, :], ALU.pow), m2, ready, price=POW)
        yield False
        for t in range(TT):
            xn = dve.do(lambda e, t=t: e.tensor_scalar(y[:, t, :], x[:, t, :], mv[:, t, 0:1],
                                                       rstd[:, t:t + 1], ALU.subtract, ALU.mult),
                        r, m2, tok_read[buf])
            if t % 2 == 1:
                yield False
        if layer == 0:
            srcT_ready[bi] = yield from transpose_block(y, xn, srcT[buf], (srcT_read[buf],))
            tok_read[buf] = (pe.counter, pe.counter.n)
            return
        normT_ready[bi] = yield from transpose_block(y, xn, normT, (state["normT_read"],))
        turned_all = (pe.counter, pe.counter.n)
        state["biased", bi] = pool.do(lambda e: e.tensor_tensor(x[:], x[:], bcon[:].rearrange(
            "p (o d) -> p o d", o=1).to_broadcast((P, TT, D)), ALU.add), xn, state["bcon_ready"], price=POOL_PASS * 4)
        S = lambda i: small[:, i, :]
        for t in range(TT):
            cl = dve.do(lambda e, t=t: e.tensor_scalar(y[:, t, :], y[:, t, :], 8.0, -8.0, ALU.min, ALU.max),
                        turned_all, xn)
            if t % 2 == 1:
                yield False
        for t in range(TT):
            m = dve.do(lambda e, t=t: e.scalar_tensor_tensor(
                out=gated[:, 0:D - 1], in0=y[:, t, 1:D], scalar=1.0, in1=y[:, t, 1:D], op0=ALU.mult,
                op1=ALU.mult, accum_out=small[:, 0, t:t + 1]), cl, state["gated_read"])
            state["gated_read"] = m
            if t % 2 == 1:
                yield False
        m = dve.do(lambda e: e.tensor_scalar(S(1), S(0), 1.0, EPS, ALU.add, ALU.add), m, price=TINY)
        m = pool.do(lambda e: e.tensor_tensor(S(2), S(1), power[:, 1, :], ALU.pow), m, price=POW)
        yield False
        m = dve.do(lambda e: e.tensor_scalar(S(3), S(2), 1.0 + EPS, None, ALU.max), m, price=TINY)
        m = dve.do(lambda e: e.tensor_scalar(S(4), S(3), 1.0, None, ALU.subtract), m, price=TINY)
        m = dve.do(lambda e: e.scalar_tensor_tensor(out=S(5), in0=S(3), scalar=1.0, in1=S(4),
                                                    op0=ALU.add, op1=ALU.mult), m, price=TINY)
        m = pool.do(lambda e: e.tensor_tensor(S(6), S(5), power[:, 1, :], ALU.pow), m, price=POW)
        m5 = dve.do(lambda e: e.tensor_tensor(S(7), S(2), S(3), ALU.subtract), m, price=TINY)
        yield False
        m = dve.do(lambda e: e.tensor_tensor(S(6), S(6), S(3), ALU.add), m, price=TINY)
        ln = act.do(lambda e: e.activation(S(8), S(6), ACT.Ln), m)
        m = dve.do(lambda e: e.tensor_tensor(S(9), S(7), S(7), ALU.mult), m5, price=TINY)
        m = dve.do(lambda e: e.tensor_tensor(S(9), S(0), S(9), ALU.subtract), m, price=TINY)
        m = dve.do(lambda e: e.tensor_scalar(S(9), S(9), EPS, None, ALU.max), m, price=TINY)
        m = pool.do(lambda e: e.tensor_tensor(S(10), S(9), power[:, 1, :], ALU.pow), m, price=POW)
        yield False
        m = dve.do(lambda e: e.tensor_scalar(S(10), S(10), EPS, None, ALU.add), m, price=TINY)
        m = dve.do(lambda e: e.reciprocal(S(10), S(10)), m, price=TINY)
        m = dve.do(lambda e: e.scalar_tensor_tensor(out=S(11), in0=S(8), scalar=1e-3, in1=S(10),
                                                    op0=ALU.max, op1=ALU.mult), m, ln, price=TINY)
        yield False
        for t in range(TT):
            v = dve.do(lambda e, t=t: e.tensor_scalar(y[:, t, 1:D], y[:, t, 1:D], small[:, 11, t:t + 1],
                                                      None, ALU.mult), m)
            if t % 2 == 1:
                yield False
        v = dve.do(lambda e: e.tensor_tensor(y[:, :, 0:1], S(7).rearrange("p (t o) -> p t o", o=1),
                                             S(11).rearrange("p (t o) -> p t o", o=1), ALU.mult), m)
        srcT_ready[bi] = yield from transpose_block(y, v, srcT[buf], (srcT_read[buf],))
        tok_read[buf] = (pe.counter, pe.counter.n)

    def values_job(bi):
        layer, _ = blocks[bi]
        buf = bi % 2
        w = w0v if layer == 0 else w1v
        for t in range(0, TT, 2):
            for i in range(2):
                for c in range(KC):
                    m = mm(chain_bank[:, i * D:(i + 1) * D], srcT[buf][:, c, (t + i) * P:(t + i + 1) * P],
                           w[:, c, :], c == 0, c == KC - 1, free["chain"], srcT_ready[bi], all_weights,
                           done=(i == 1 and c == KC - 1))
                    yield True
            view = values[buf][:, t:t + 2, :, 0:HS]
            src = chain_bank[:].rearrange("p (t h d) -> p t h d", t=2, h=H)
            if layer == 0:
                last = dve.do(lambda e, view=view, src=src: e.tensor_tensor(
                    view, src, b0v[:].rearrange("p (o h d) -> p o h d", o=1, h=H).to_broadcast((P, 2, H, HS)), ALU.add),
                    m, values_read[buf], ready, all_weights, price=DVE_PASS)
            else:
                last = act.do(lambda e, view=view, src=src: e.copy(view, src), m, values_read[buf], ready)
            free["chain"] = last
            yield False
        values_ready[bi] = last
        srcT_read[buf] = m

    def router_job(bi):
        buf = bi % 2
        G = gate_w[buf]
        for t in range(TT):
            for c in range(KC):
                m = mm(chain_bank[:, t * NE:(t + 1) * NE], srcT[buf][:, c, t * P:(t + 1) * P], rw[:, c, :],
                       c == 0, c == KC - 1, free["chain"], srcT_ready[bi], all_weights,
                       done=(t == TT - 1 and c == KC - 1))
        srcT_read[buf] = m
        yield True
        rb_all = rb[:].rearrange("p (o n) -> p o n", o=1).to_broadcast((P, TT, NE))
        lg = dve.do(lambda e: e.tensor_tensor(logit[:], chain_bank[:, 0:TT * NE].rearrange(
            "p (t n) -> p t n", t=TT), rb_all, ALU.add), m, all_weights)
        free["chain"] = lg
        yield False
        mx = dve.do(lambda e: e.tensor_reduce(lmax[:], logit[:], AX, ALU.max), lg, price=TINY)
        bc = lambda v: v[:].rearrange("p (t o) -> p t o", o=1).to_broadcast((P, TT, NE))
        sh = dve.do(lambda e: e.tensor_tensor(lwork[:], logit[:], bc(lmax), ALU.subtract), mx, price=TINY)
        ex = act.do(lambda e: e.activation(logit[:], lwork[:], ACT.Exp), sh)
        eq = dve.do(lambda e: e.tensor_scalar(lwork[:], lwork[:], 0.0, None, ALU.is_equal), ex, price=TINY)
        eq = dve.do(lambda e: e.tensor_tensor(lwork[:], lwork[:], first_wins[:], ALU.mult), eq, ready, price=TINY)
        fm = dve.do(lambda e: e.tensor_reduce(lmax[:], lwork[:], AX, ALU.max), eq, price=TINY)
        yield False
        oh = dve.do(lambda e: e.tensor_tensor(lwork[:], lwork[:], bc(lmax), ALU.is_equal), fm, price=TINY)
        sm = dve.do(lambda e: e.tensor_reduce(lsum[:], logit[:], AX, ALU.add), ex, price=TINY)
        sm = dve.do(lambda e: e.reciprocal(lsum[:], lsum[:]), sm, price=TINY)
        gw = dve.do(lambda e: e.tensor_tensor(G[:], lwork[:], bc(lsum), ALU.mult), oh, sm, state["gate_read"][buf], price=TINY)
        state["gate_ready", bi] = gw
        yield False

    last_expert = (blocks.index((0, NB - 1)), NE - 1)

    def load_expert(ex):
        return load(w_expert[ex % 2][:], a["expert_w"][ex], expert_in[ex % 2], state["experts"][ex % 2])

    def next_bulk():
        state["bulk"] = i = 1 - state.get("bulk", 1)
        return i, bulk_banks[i]

    def experts_job(bi, quarter):
        buf = bi % 2
        for ex in range(2 * quarter, 2 * quarter + 2):
            s = ex % 2
            win = state["expert_win"]
            for t in range(0, TT, 2):
                bk_i, bulk = next_bulk()
                for i in range(2):
                    for c in range(KC):
                        m = mm(bulk[:, i * D:(i + 1) * D], srcT[buf][:, c, (t + i) * P:(t + i + 1) * P],
                               w_expert[s][:, c, :], c == 0, c == KC - 1, free[bk_i], win,
                               srcT_ready[bi], done=(i == 1 and c == KC - 1))
                        yield True
                state["experts"][s] = m
                for i in range(2):
                    key = ("moe", bi, t + i)
                    last = dve.do(lambda e, i=i, t=t, ex=ex, bulk=bulk: e.scalar_tensor_tensor(
                        out=acc[buf][:, t + i, :], in0=bulk[:, i * D:(i + 1) * D],
                        scalar=gate_w[buf][:, t + i, ex:ex + 1], in1=acc[buf][:, t + i, :],
                        op0=ALU.mult, op1=ALU.add), m, state["gate_ready", bi], state.get(key))
                    state[key] = last
                free[bk_i] = last
                if t == 0 and (bi, ex) != last_expert:
                    state["expert_win"] = load_expert((ex + 1) % NE)
                yield False
        srcT_read[buf] = m
        acc_ready[bi] = last

    def quad_job(n):
        bi, quad = divmod(n, NQ)
        layer, _ = blocks[bi]
        buf, slot = bi % 2, n % 3
        w = w0qk if layer == 0 else w1qk
        q0 = 0 if quad % 2 == 0 else 64
        k0 = 64 - q0
        if layer == 1:
            yield False, lambda: (bi, quad // 2, "all") in metric_ready
        for half in range(2):
            cols = slice(half * HALF, (half + 1) * HALF)
            for c in range(KC):
                m = mm(chain_bank[:], w[:, c, quad, :], srcT[buf][:, c, cols], c == 0, c == KC - 1,
                       free["chain"], srcT_ready[bi], all_weights, done=(c == KC - 1))
                yield True
            if layer == 0:
                bias = b0qk[:, quad:quad + 1]
                hi = act.do(lambda e, cols=cols, bias=bias: e.activation(
                    part[0][:, cols], chain_bank[:], ACT.Identity, bias=bias), m, state["parts_read"], all_weights)
                r = dve.do(lambda e, cols=cols, bias=bias: e.scalar_tensor_tensor(
                    out=rest[:], in0=chain_bank[:], scalar=bias, in1=part[0][:, cols],
                    op0=ALU.add, op1=ALU.subtract), hi, state["rest_read"], price=DVE_PASS)
                free["chain"] = r
            else:
                g = metric[q0:q0 + 64, quad // 2, cols]
                a1 = dve.do(lambda e, g=g: e.tensor_tensor(gated[q0:q0 + 64, :], chain_bank[q0:q0 + 64, :], g,
                                                           ALU.mult), m, metric_ready[bi, quad // 2], state["gated_read"], price=DVE_PASS)
                a2 = act.do(lambda e: e.copy(gated[k0:k0 + 64, :], chain_bank[k0:k0 + 64, :]), m, state["gated_read"])
                state["metric_read"][quad // 2] = a1
                hi = dve.do(lambda e, cols=cols: e.tensor_copy(part[0][:, cols], gated[:]), a1, a2, state["parts_read"])
                free["chain"] = hi
                r = pool.do(lambda e, cols=cols: e.tensor_tensor(rest[:], gated[:], part[0][:, cols], ALU.subtract),
                            hi, state["rest_read"], price=POOL_PASS)
                state["gated_read"] = r
            mid = pool.do(lambda e, cols=cols: e.tensor_scalar(part[1][:, cols], rest[:], 1.0, 0.0, ALU.mult, ALU.add),
                          r, state["parts_read"])
            lo = pool.do(lambda e, cols=cols: e.tensor_tensor(part[2][:, cols], rest[:], part[1][:, cols], ALU.subtract),
                         mid, state["parts_read"], price=POOL_PASS)
            state["rest_read"] = lo
            yield False
        srcT_read[buf] = m
        for i, (pq, pk) in enumerate(zip(Q_ORDER, K_ORDER)):
            rows = slice(i * BLK, (i + 1) * BLK)
            load(qstack[slot][rows, :, :], part[pq][q0:q0 + 64, :], stack_in[slot], hi, lo, stack_read[slot])
            mark = load(kstack[slot][rows, :, :], part[pk][k0:k0 + 64, :], stack_in[slot])
        stack_ready[n] = mark
        state["parts_read"] = mark
        yield False

    def metric_job(bi):
        hidden = hid[:].rearrange("p (m n) -> p m n", m=MT)
        yield False, lambda: bi in normT_ready
        for half in range(2):
            cols = slice(half * HALF, (half + 1) * HALF)
            for mt in range(MT):
                bk_i, bulk = next_bulk()
                for c in range(KC):
                    m = mm(bulk[:], wm1[:, c, mt * P:(mt + 1) * P], normT[:, c, cols], c == 0, c == KC - 1,
                           free[bk_i], normT_ready[bi], all_weights, done=(c == KC - 1))
                    yield True
                th = act.do(lambda e, mt=mt, bulk=bulk: e.activation(hidden[:, mt, :], bulk[:], ACT.Tanh,
                                                          bias=bm1[:, mt:mt + 1]), m, state["hid_read"], state["bm1_ready"], *state["butterfly_done"])
                free[bk_i] = th
                yield False
            for pair in range(2):
                bk_i, bulk = next_bulk()
                for kt in range(MT):
                    m = mm(bulk[:], wm2[:, kt, pair, :], hidden[:, kt, :], kt == 0, kt == MT - 1,
                           free[bk_i], th, done=(kt == MT - 1))
                    yield True
                g = metric[:, pair, cols]
                t2 = act.do(lambda e, g=g, pair=pair, bulk=bulk: e.activation(g, bulk[:], ACT.Tanh, bias=bm2[:, pair:pair + 1]),
                            m, state["metric_read"][pair])
                free[bk_i] = t2
                metric_ready[bi, pair] = dve.do(lambda e, g=g, pair=pair: e.tensor_scalar(
                    g, g, 0.1, eta[:, pair:pair + 1], ALU.mult, ALU.add), t2, ready)
                if half == 1:
                    metric_ready[bi, pair, "all"] = True
                yield False
            state["hid_read"] = m
        state["normT_read"] = m

    def ffn_job(bi, quarters):
        buf = bi % 2
        Q = T // 4
        hidden = hid[:].rearrange("p (h n) -> p h n", h=HT)
        for q in quarters:
            cols = slice(q * Q, (q + 1) * Q)
            for ht in range(0, HT, 2):
                bk_i, bulk = next_bulk()
                for i in range(2):
                    for c in range(KC):
                        m = mm(bulk[:, i * Q:(i + 1) * Q], wexp[:, c, (ht + i) * P:(ht + i + 1) * P],
                               normT[:, c, cols], c == 0, c == KC - 1, free[bk_i], normT_ready[bi],
                               state["ffn_ready"], state["ffn_ready1"], state["ffn_ready2"], done=(i == 1 and c == KC - 1))
                        yield True
                ev = dve.do(lambda e, ht=ht, bulk=bulk: e.tensor_tensor(
                    hidden[:, ht:ht + 2, :], bulk[:].rearrange("p (h n) -> p h n", h=2),
                    bexp[:, ht:ht + 2].rearrange("p (h o) -> p h o", o=1).to_broadcast((P, 2, Q)), ALU.add),
                    m, state["hid_read"], state["ffn_bias"], price=DVE_PASS)
                free[bk_i] = ev
                yield False
            state["normT_read"] = m
            ge = act.do(lambda e: e.activation(hid[:], hid[:], ACT.Gelu), ev, price=1800 + TABLE)
            act.clock += TABLE
            yield False
            bk_i, bulk = next_bulk()
            for i in range(2):
                for ht in range(HT):
                    m = mm(bulk[:, i * D:(i + 1) * D], hidden[:, ht, i * P:(i + 1) * P], wcon[:, ht, :],
                           ht == 0, ht == HT - 1, free[bk_i], ge, done=(i == 1 and ht == HT - 1))
                    yield True
            state["hid_read"] = m
            view = acc[buf][:, 2 * q:2 * q + 2, :]
            last = dve.do(lambda e, view=view, bulk=bulk: e.tensor_tensor(view, bulk[:].rearrange("p (t d) -> p t d", t=2),
                                                               view, ALU.add), m, state["biased", bi], price=DVE_PASS)
            free[bk_i] = last
            yield False
        acc_ready[bi] = last

    butterfly_in, wcon_in = [sem("butterfly_in0"), sem("butterfly_in1")], sem("wcon_in")

    def butterfly_job():
        order = [("up", stage) for stage in range(STAGES)] + [("down", stage) for stage in reversed(range(STAGES))]

        def load_stage(k, *read):
            which, stage = order[k]
            return load(bf_w[k % 2], a[which][stage].rearrange("(o c) j -> o c j", o=1).to_broadcast(
                (P, 4, FH // 2)), butterfly_in[k % 2], *read, lag=BIG_LOAD)

        win = load_stage(0)
        done, read = (all_weights, all_weights), ()
        for k in range(STAGES):
            after = load_stage(k + 1, *read)
            done = read = yield from butterfly_stage(
                order[k][1], ((pool, wexp[:, 0, :]), (dve, wexp[:, 1, :]), (dve, bias_row)), (0, 1, 2, 3),
                bf_w[k % 2], win, done, read)
            win = after
        state["ffn_ready"], state["ffn_ready1"] = done
        for ht in range(HT):
            m = pe.do(lambda e, ht=ht: e.transpose(chain_bank[:, ht:ht + 1], bias_row[0:1, ht * P:(ht + 1) * P],
                                                   ident[0:1, 0:1]), free["chain"], state["ffn_ready1"],
                      signal=(ht == HT - 1))
        yield True
        state["ffn_bias"] = dve.do(lambda e: e.tensor_tensor(bexp[:], chain_bank[:, 0:HT], upb[:], ALU.add), m, all_weights)
        free["chain"] = state["ffn_bias"]
        state["bcon_ready"] = dve.do(lambda e: e.tensor_tensor(bcon[:], bcon[:], dbias, ALU.add), all_weights)
        wt_in = wcon_in
        held = [normT[:, i, :] for i in range(KC)]
        for i in range(KC):
            dn = load(held[i], a["wconT"][i * P:(i + 1) * P, :], wt_in, m, state["bcon_ready"])
        done = (dn, dn)
        for k in range(STAGES, 2 * STAGES):
            after = load_stage(k + 1, *read) if k + 1 < 2 * STAGES else None
            done = read = yield from butterfly_stage(
                order[k][1], ((pool, held[0]), (dve, held[1])), (0, 2, 1, 3), bf_w[k % 2], win, done, read)
            win = after
        for ht in range(0, HT, 2):
            for i in range(2):
                for tile in range(KC):
                    m = pe.do(lambda e, i=i, tile=tile, ht=ht: e.transpose(
                        chain_bank[:, (i * 2 + tile) * P:(i * 2 + tile + 1) * P],
                        held[tile][:, (ht + i) * P:(ht + i + 1) * P], ident[:]), free["chain"], *done, id_ready,
                        signal=(i == 1 and tile == 1))
            yield True
            last = act.do(lambda e, ht=ht: e.copy(wcon[:, ht:ht + 2, :], chain_bank[:].rearrange("p (h d) -> p h d", h=2)), m)
            free["chain"] = last
            yield False
        state["normT_read"] = m
        state["ffn_ready2"] = last
        state["bm1_ready"] = dve.do(lambda e: e.tensor_tensor(bm1[:], bm1[:], wm1c[:], ALU.subtract), all_weights, price=TINY)
        state["butterfly_done"] = read
        yield False

    def butterfly_stage(stage, tiles, order, weights, win, done, before):
        s = 2 ** stage
        result = {}
        yield False, win
        for half in range(2):
            for lane, rows in tiles:
                p = rows.shape[0]
                y = rows.rearrange("p (n a s) -> p n a s", a=2, s=s)
                n, w = y.shape[1], min(s, HALF // 2)
                ns = slice(half * n // 2, (half + 1) * n // 2) if n > 1 else slice(0, 1)
                ss = slice(0, s) if n > 1 else slice(half * w, (half + 1) * w)
                va, vb = y[:, ns, 0, ss], y[:, ns, 1, ss]
                t = bf_t[:, 0:2, :] if lane is pool else bf_t[:, 2:4, :]
                t = t.rearrange("p a b -> p (a b)").rearrange("p (i n s) -> p i n s", i=4, s=w)
                wt = weights[:, :, half * HALF // 2:(half + 1) * HALF // 2].rearrange("p i (n s) -> p i n s", s=w)
                ydone = done[0] if lane is pool else done[1]
                for i, src in enumerate((va, vb, va, vb)):
                    m = lane.do(lambda e, i=i, src=src, t=t, wt=wt, p=p: e.tensor_tensor(
                        t[0:p, i], src, wt[0:p, order[i]], ALU.mult), win, ydone, result.get(lane.name), *before)
                    if i % 2 == 1:
                        yield False
                lane.do(lambda e, t=t, va=va, p=p: e.tensor_tensor(va, t[0:p, 0], t[0:p, 1], ALU.add), m)
                result[lane.name] = lane.do(lambda e, t=t, vb=vb, p=p: e.tensor_tensor(
                    vb, t[0:p, 2], t[0:p, 3], ALU.add), m)
                yield False
        return result["pool"], result["dve"]

    def load_job(bi):
        layer, b = blocks[bi]
        buf = bi % 2
        src = x_dram[b] if layer == 0 else x1_dram[b]
        acc_loaded[bi] = load(acc[buf][:], src, x_in[buf], state.get(("stored", buf)),
                              state["x1"].get(b) if layer == 1 else None, lag=BIG_LOAD)
        yield False

    def finish_job(bi):
        layer, b = blocks[bi]
        buf = bi % 2
        O = tok[buf]
        w = w0o if layer == 0 else w1o
        for t in range(0, TT, 2):
            if layer == 0 and t % 4 == 0:
                for i in range(4):
                    m = pe.do(lambda e, i=i, t=t: e.transpose(
                        chain_bank[0:NE, i * P:(i + 1) * P], gate_w[buf][:, t + i, :], ident[:]),
                        free["chain"], state["gate_ready", bi], id_ready, signal=(i == 3))
                state["gate_read"][buf] = m
                yield True
                gates = dve.do(lambda e: e.tensor_copy(gateT[0:NE, :], chain_bank[0:NE, :]), m, state["gateT_read"], price=DVE_PASS)
                free["chain"] = gates
                yield False
            for i in range(4):
                m = pe.do(lambda e, i=i, t=t: e.transpose(
                    chain_bank[:, i * P:(i + 1) * P], O[:, t + i // 2, (i % 2) * P:(i % 2 + 1) * P], ident[:]),
                    free["chain"], heads_out[bi], signal=(i == 3))
            tok_read[buf] = m
            yield True
            ev = act.do(lambda e: e.copy(turned[:], chain_bank[:]), m, state["turned_read"])
            free["chain"] = ev
            yield True
            for i in range(2):
                for c in range(KC):
                    last = layer == 1 and c == KC - 1
                    m = mm(chain_bank[:, i * D:(i + 1) * D], turned[:, (2 * i + c) * P:(2 * i + c + 1) * P], w[:, c, :],
                           c == 0, last, ev, free["chain"], done=(last and i == 1))
                    yield True
                if layer == 0:
                    m = mm(chain_bank[:, i * D:(i + 1) * D], gateT[:, (t % 4 + i) * P:(t % 4 + i + 1) * P], expert_b[:],
                           False, True, gates, done=(i == 1))
            state["turned_read"] = m
            if layer == 0:
                state["gateT_read"] = m
            yield True
            view = acc[buf][:, t:t + 2, :]
            pv = chain_bank[:].rearrange("p (t d) -> p t d", t=2)
            if layer == 0:
                last = dve.do(lambda e, view=view, pv=pv: e.tensor_tensor(view, pv, view, ALU.add), m, acc_ready[bi],
                              price=DVE_PASS)
                free["chain"] = last
            else:
                g2 = gated[:].rearrange("p (t d) -> p t d", t=2)
                z = dve.do(lambda e: e.tensor_scalar(gated[:], chain_bank[:], 0.1, 8.0, ALU.mult, ALU.min), m, state["gated_read"])
                free["chain"] = z
                z = dve.do(lambda e: e.tensor_scalar(gated[:], gated[:], -8.0, None, ALU.max), z)
                for i in range(2):
                    sq = dve.do(lambda e, i=i: e.scalar_tensor_tensor(
                        out=rest[:, 0:D - 1], in0=g2[:, i, 1:D], scalar=1.0, in1=g2[:, i, 1:D], op0=ALU.mult,
                        op1=ALU.mult, accum_out=zsum[:, i:i + 1]), z, state["rest_read"])
                    state["rest_read"] = sq
                sq = dve.do(lambda e: e.tensor_scalar(zsum[:], zsum[:], 1.0, EPS, ALU.add, ALU.add), sq, price=TINY)
                x0 = pool.do(lambda e: e.tensor_tensor(g2[:, :, 0:1], zsum[:].rearrange("p (t o) -> p t o", o=1),
                                                       power[:, 1, 0:2].rearrange("p (t o) -> p t o", o=1), ALU.pow), sq, z, price=POW)
                yield True
                last = dve.do(lambda e, view=view, g2=g2: e.tensor_tensor(view, g2, view, ALU.add), x0, acc_ready[bi])
                state["gated_read"] = last
            dst = x1_dram[b] if layer == 0 else out_dram[b]
            store = sp.do(lambda e, view=view, dst=dst, t=t: e.dma_start(dst[:, t:t + 2, :], view), last,
                          done=acc_out[buf], by=16)
            yield False
        state[("stored", buf)] = store
        if layer == 0:
            state["x1"][b] = store

    zsum = sb("zsum", [P, 2])

    def heads_job(n, hq):
        bi, quad = divmod(n, NQ)
        O = tok[bi % 2]
        yield False, state["headsT"]
        for i in range(4):
            m = pe.do(lambda e, i=i: e.transpose(chain_bank[:, i * P:(i + 1) * P], headsT[:, i * P:(i + 1) * P], ident[:]),
                      free["chain"], state["headsT"], signal=(i == 3))
        state["headsT_read"] = m
        state["heads_taken"] = True
        yield True
        bk = chain_bank[:].rearrange("p (t h r) -> p t h r", t=4, h=QH)
        rc = dve.do(lambda e: e.reciprocal(recip[:].rearrange("p t (h o) -> p t h o", o=1), bk[:, :, :, HS:HS + 1]),
                    m, state["recip"])
        dst = O[:, hq * 4:hq * 4 + 4, quad * 64:(quad + 1) * 64].rearrange("p t (h d) -> p t h d", h=QH)
        last = dve.do(lambda e: e.tensor_tensor(dst, bk[:, :, :, 0:HS], recip[:].rearrange(
            "p t (h o) -> p t h o", o=1).to_broadcast((P, 4, QH, HS)), ALU.mult), rc, tok_read[bi % 2])
        state["recip"] = last
        free["chain"] = last
        heads_out[bi] = last
        yield False

    def maxes_job(n):
        slot, mb = n % 3, n % 2
        M = maxes[mb]
        m = dve.do(lambda e: e.tensor_tensor(negmax[:].rearrange("p (h t) -> p h t", h=QH), M[:, 0, :, :],
                                             M[:, 1, :, :], ALU.min), (dve_max, dve_max.n), state.get("negmax_read"))
        maxes_read[mb] = m
        yield False
        m = pe.do(lambda e: e.transpose(chain_bank[0:QH * TT, 0:P], negmax[:], ident[:]), m, free["chain"])
        state["negmax_read"] = m
        yield True
        mp = mpart[mb]
        src = chain_bank[0:QH * TT, 0:P]
        h = dve.do(lambda e: e.tensor_copy(mp[:, 0, :], src), m, state["mpart"])
        r = dve.do(lambda e: e.tensor_tensor(mrest[:], src, mp[:, 0, :], ALU.subtract), h)
        free["chain"] = r
        md = dve.do(lambda e: e.tensor_copy(mp[:, 1, :], mrest[:]), r)
        lo = dve.do(lambda e: e.tensor_tensor(mp[:, 2, :], mrest[:], mp[:, 1, :], ALU.subtract), md)
        for i in range(3):
            mark = load(qstack[slot][SROWS + i:SROWS + i + 1, :, :], mp[:, i, :], stackm_in[slot], lo, stack_read[slot])
        stackm_ready[n] = mark
        state["mpart"] = mark
        yield False

    def first_pass(n):
        bi, _ = divmod(n, NQ)
        layer, _ = blocks[bi]
        slot, M = n % 3, maxes[n % 2]
        if layer == 0:
            dve.do(lambda e: e.memset(M[:, 1, :, 0:4], BIG), maxes_read[n % 2], done=dve_max)
        for j in range(QH):
            for t in range(TT):
                for half in range(2):
                    width = HALF
                    if layer == 0:
                        width = min(HALF, (t + 1) * P - half * HALF)
                        if width <= 0:
                            continue
                    i = first_pass.count % 2
                    first_pass.count += 1
                    bk = max_bank[i]
                    diag = layer == 0 and half == t // 4
                    m = mm(bk[:, 0:width], qstack[slot][0:SROWS, j, t * P:(t + 1) * P],
                           kstack[slot][0:SROWS, j, half * HALF:half * HALF + width], True, not diag,
                           stack_ready[n], max_free[i], done=not diag, counter=pe_max)
                    if diag:
                        m = mm(bk[:, width - P:width], ident_bf[:], causal[:], False, True, causal_ready,
                               done=True, counter=pe_max)
                    max_free[i] = dve.do(lambda e, bk=bk, width=width, half=half, j=j, t=t: e.tensor_reduce(
                        M[:, half, j, t:t + 1], bk[:, 0:width], AX, ALU.max, negate=True), m, maxes_read[n % 2],
                        done=dve_max, price=65 + width / 0.96)
                    yield
    first_pass.count = 0

    def second_pass(n):
        bi, quad = divmod(n, NQ)
        layer, _ = blocks[bi]
        slot = n % 3
        pe.wait(k_ones)
        for hq in range(2):
            nk = TT if layer == 1 or hq == 1 else 4
            for kt in range(nk):
                c0 = max(0, kt * P - hq * HALF) if layer == 0 else 0
                pb = second_pass.count % 2
                second_pass.count += 1
                for j in range(QH):
                    i = j % 2
                    m = mm(score_bank[i][:, c0:HALF], kstack[slot][0:SROWS + MROWS, j, kt * P:(kt + 1) * P],
                           qstack[slot][0:SROWS + MROWS, j, hq * HALF + c0:(hq + 1) * HALF], True, True,
                           score_free[i], stack_ready[n], stackm_ready[n], done=True, counter=pe_scores)
                    e_ = act.do(lambda e, i=i, j=j, c0=c0, pb=pb: e.activation(prob[pb][:, j, c0:HALF],
                                score_bank[i][:, c0:HALF], ACT.Exp, scale=SCALE), m, second_pass.read[pb], done=act_exp,
                                price=50 + (HALF - c0) / 1.2)
                    score_free[i] = e_
                    if j == 2 and second_pass.pending:
                        second_pass.next = second_pass.pending[-1]
                        yield None
                        second_pass.next = score_free[1 - i]
                        yield product(*second_pass.pending)
                    elif j < QH - 1:
                        second_pass.next = score_free[1 - i]
                        yield None
                masked = e_
                if layer == 0 and kt * P >= hq * HALF:
                    view = prob[pb][:, :, c0:c0 + P]
                    masked = pool.do(lambda e, view=view: e.affine_select(
                        out=view, in_=view, compare_op=ALU.is_ge, fill=0.0, base=0,
                        pattern=[[0, QH], [1, P]], channel_multiplier=-1), e_)
                second_pass.pending = (n, hq, kt, nk, c0, pb, masked)
                second_pass.next = score_free[0]
                yield None
        stack_read[slot] = (pe_scores, pe_scores.n)

    def product(n, hq, kt, nk, c0, pb, masked):
        bi, quad = divmod(n, NQ)
        V = values[bi % 2]
        for j in range(QH):
            m = pe.do(lambda e, j=j: e.matmul(pv_bank[32 * j:32 * j + VC, c0:HALF], V[:, kt, QH * quad + j, :],
                                              prob[pb][:, j, c0:HALF], start=(kt == 0), stop=(kt == nk - 1)),
                      masked, values_ready[bi], free["pv"] if kt == 0 else None, signal=(j == QH - 1), price=(HALF - c0) * 1.05 / 2.4)
        second_pass.read[pb] = values_read[bi % 2] = m
        second_pass.pending = None
        if kt < nk - 1:
            return None
        assert state.get("heads_taken", True)
        state["heads_taken"] = False
        state["headsT"] = free["pv"] = act.do(lambda e: e.copy(headsT[:], pv_bank[:]), m, state.get("headsT_read"))
        return n, hq
    second_pass.count, second_pass.read, second_pass.pending, second_pass.next = 0, [None, None], None, None

    class Stream:

        def __init__(self):
            self.jobs, self.urgent, self.held, self.now, self.wake = [], [], False, None, 0.0
            self.may_stay = None

        def step(self):
            if self.now is None or (not self.held and self.urgent and not self.now[1]):
                if self.urgent:
                    if self.now is not None:
                        self.jobs.insert(0, self.now[0])
                    self.now = (self.urgent.pop(0), True)
                elif self.jobs:
                    self.now = (self.jobs.pop(0), False)
                else:
                    return False
            try:
                self.held = next(self.now[0])
                self.wake = Lane.wake
                if isinstance(self.held, tuple):
                    self.held, self.wake = self.held
                    if not callable(self.wake):
                        self.wake = when(self.wake)
            except StopIteration:
                self.now, self.held = None, False
            return True

        def hurry(self):
            return (self.now[1] if self.now else False) or (bool(self.urgent) and not self.held)

        def empty(self):
            return self.now is None and not self.jobs and not self.urgent

        def settled(self):
            return self.empty() or (not self.urgent and not self.held and self.may_stay is not None and
                                    (self.now[0] if self.now else self.jobs[0]) is self.may_stay)

        def drain(self):
            while not self.settled():
                self.step()

    chain, bulk = Stream(), Stream()
    norm = [None]
    butter_credit, butter_wake = [0.0], [0.0]

    def jobs_of(period):
        bi, q = divmod(period, NQ)
        cj, bj = [], []
        if period + 2 < NP_:
            cj.append(quad_job(period + 2))
        nb = bi + 1
        two_in_a_row = nb < NBL and blocks[bi][0] == 1 and blocks[nb][0] == 1
        if q == two_in_a_row and nb < NBL:
            norm[0] = norm_job(nb)
            cj.append(norm[0])
        if q == 1 and nb < NBL:
            if blocks[nb][0] == 0:
                cj.append(router_job(nb))
            cj.append(values_job(nb))
        if q in (2, 3) and nb < NBL:
            bj.append(ffn_job(nb, (q - 2,)) if blocks[nb][0] == 1 else experts_job(nb, q - 2))
        if q == 0:
            bj.append(ffn_job(bi, (2, 3) if two_in_a_row else (2,)) if blocks[bi][0] == 1 else experts_job(bi, 2))
        if q == 1 and not two_in_a_row:
            bj.append(ffn_job(bi, (3,)) if blocks[bi][0] == 1 else experts_job(bi, 3))
        if q == 1 and nb < NBL and blocks[nb][0] == 1:
            bj.append(metric_job(nb))
        return cj, bj

    def run_all(*jobs):
        for g in jobs:
            for _ in g:
                pass

    state["expert_win"] = load_expert(0)
    run_all(norm_job(0))
    for i in range(3):
        pool.wait((pool.counter, pool.counter.n))
        k_ones = pool.do(lambda e, i=i: e.memset(kstack[i][SROWS:SROWS + MROWS, :, :], 1.0))
    pool.wait(k_ones)
    run_all(router_job(0), quad_job(0), load_job(1))

    butter = [butterfly_job()]
    did = {}
    bulk.jobs += [experts_job(0, 0), experts_job(0, 1)]
    chain.jobs += [values_job(0), quad_job(1)]
    for i, _ in enumerate(first_pass(0)):
        for _ in range(2 + i % 2):
            (bulk if i % 3 else chain).step()
    chain.drain()
    run_all(maxes_job(0))
    for period in range(NP_):
        bi, q = divmod(period, NQ)
        cj, bj = jobs_of(period)
        chain.jobs += cj
        bulk.jobs += bj
        atten = second_pass(period)
        first = first_pass(period + 1) if period + 1 < NP_ else iter(())

        def step_second():
            ev = next(atten, "end")
            if ev == "end":
                return False
            if ev is not None:
                chain.urgent.append(heads_job(*ev))
                n, hq = ev
                if hq == 1 and n % NQ == NQ - 1:
                    chain.jobs.insert(0, finish_job(n // NQ))
                    if n // NQ + 2 < NBL:
                        chain.jobs.insert(1, load_job(n // NQ + 2))
            return True

        def step_first():
            if next(first, "end") == "end":
                if period + 1 < NP_:
                    chain.urgent.append(maxes_job(period + 1))
                return False
            return True

        def step_butterfly():
            if not butter or chain.held:
                return bool(butter)
            held = next(butter[0], "end")
            while held is True:
                held = next(butter[0], "end")
            butter_wake[0] = 0.0
            if isinstance(held, tuple):
                butter_wake[0] = when(held[1])
            if held == "end":
                butter.clear()
                return False
            return True

        steps = {"second": step_second, "first": step_first, "chain": chain.step, "bulk": bulk.step}
        ahead = {"second": 1.0, "first": FIRST_AHEAD, "chain": CHAIN_EARLY if q < 2 else CHAIN_AHEAD, "bulk": 1.0}
        live, work = dict(steps), dict.fromkeys(steps, 0.0)
        def ready_at(s):
            if s == "second":
                return when(second_pass.next)
            if s == "first":
                return when(max_free[first_pass.count % 2])
            wake = (chain if s == "chain" else bulk).wake
            if s == "chain" and callable(wake) and chain.urgent and not chain.held and not (chain.now and chain.now[1]):
                return 0.0
            return (0.0 if wake() else INFINITE) if callable(wake) else wake

        chain.may_stay = norm[0] if q == 0 else None
        while live and (any(s in live for s in ("second", "first")) or not chain.settled() or not bulk.settled()):
            def progress(s):
                return work[s] / plan.get((period, s), 1.0) / ahead[s]
            startable = [s for s in live if ready_at(s) <= pe.clock + SLACK]
            s = min(startable, key=progress) if startable else min(live, key=ready_at)
            if "second" in live and s != "chain" and chain.hurry() and ready_at("chain") <= pe.clock + SLACK:
                s = "chain"
            if s in ("chain", "bulk") and not ("second" in live or "first" in live) and (chain if s == "chain" else bulk).settled():
                s = "bulk" if s == "chain" else "chain"
            before = Lane.cost
            fn = steps[s]
            if not fn():
                if s in live:
                    del live[s]
            work[s] += max(Lane.cost - before, 1.0)
            if period <= NQ and butter:
                butter_credit[0] += BUTTER_RATE
                while butter_credit[0] > 1 and butter_wake[0] <= pe.clock and step_butterfly():
                    butter_credit[0] -= 1
        for s in steps:
            did[period, s] = work[s]
        chain.drain()
        bulk.drain()
        if period == NQ - 1 and butter:
            while chain.held:
                chain.step()
            run_all(butter.pop())
    assert chain.empty() and bulk.empty()
    run_all(heads_job(*product(*second_pass.pending)), finish_job(NBL - 1))
    for c in acc_out:
        sp.wait((c, c.n))
    return did, (sp, pe, act, dve, pool)


def build(nc, aps, out):
    with ExitStack() as ctx:
        mem = Memory(nc, ctx)
        plan, _ = two_layers(mem, aps, out, {})
        plan, _ = two_layers(mem, aps, out, plan)
        _, (sp, pe, act, dve, pool) = two_layers(mem, aps, out, plan)
        with nc.Block() as block:
            block.sync(sp.run)
            block.tensor(pe.run)
            block.scalar(act.run)
            block.vector(dve.run)
            block.gpsimd(pool.run)


def kernel(**inputs):
    import concourse.bacc as bacc
    from concourse.bass_utils import run_bass_kernel_spmd

    g = {k: np.asarray(v) for k, v in inputs.items()}

    def rows(w):
        return w.reshape(w.shape[0] // P, P, -1).transpose(1, 0, 2)

    def quad_cols(w):
        w = w.reshape(*w.shape[:-1], NQ, QH, HS)
        return np.swapaxes(w, -1, -2).reshape(*w.shape[:-3], NQ, QH * HS)

    def qk_cols(q, k):
        q, k = quad_cols(q), quad_cols(k)
        even = np.concatenate([q, k], -1)
        odd = np.concatenate([k, q], -1)
        pick = [even[..., i, :] if i % 2 == 0 else odd[..., i, :] for i in range(NQ)]
        return np.stack(pick, -2)

    w0 = g["L0_attn_attn_W"].reshape(D, H, 3, HS)
    b0 = g["L0_attn_attn_b"].reshape(H, 3, HS)
    flat = lambda w: w.reshape(*w.shape[:-2], H * HS)
    w2q = quad_cols(g["L1_attn_W2"].T)
    b2q = quad_cols(g["L1_attn_b2"])
    host = {
        "x": g["L0_attn_encodings"],
        "w0qk": rows(qk_cols(flat(w0[:, :, 0]), flat(w0[:, :, 1])).reshape(D, NQ * P)).reshape(P, KC, NQ, P),
        "b0qk": qk_cols(flat(b0[:, 0]), flat(b0[:, 1])).T,
        "w0v": rows(flat(w0[:, :, 2])),
        "b0v": flat(b0[:, 2]),
        "w0o": rows(g["L0_attn_out_W"]),
        "b0o": g["L0_attn_out_b"][None, :],
        "rw": rows(g["L0_ffn_router_w"]),
        "rb": g["L0_ffn_router_b"],
        "expert_w": g["L0_ffn_expert_w"].reshape(NE, KC, P, D).transpose(0, 2, 1, 3),
        "expert_b": g["L0_ffn_expert_b"],
        "w1qk": rows(qk_cols(g["L1_attn_Wq"].T, g["L1_attn_Wk"].T).reshape(D, NQ * P)).reshape(P, KC, NQ, P),
        "w1v": rows(g["L1_attn_Wv"].T),
        "w1o": rows(g["L1_attn_Wo"].T),
        "wm1": rows(g["L1_attn_W1"].T),
        "bm1": g["L1_attn_b1"].reshape(MT, P).T,
        "wm1c": g["L1_attn_W1"][:, 0].reshape(MT, P).T,
        "wm2": w2q.reshape(MT, P, 2, P).transpose(1, 0, 2, 3),
        "bm2": b2q.reshape(2, P).T,
        "wexp": rows(g["L1_ffn_W_exp"]),
        "b_exp": g["L1_ffn_b_exp"][None, :],
        "upb": g["L1_ffn_up_bias"].reshape(HT, P).T,
        "up": g["L1_ffn_up_weights"].reshape(STAGES, FH // 2, 4).transpose(0, 2, 1),
        "down": g["L1_ffn_down_weights"].reshape(STAGES, FH // 2, 4).transpose(0, 2, 1),
        "wconT": g["L1_ffn_W_con"].T,
        "b_con": g["L1_ffn_b_con"],
        "down_bias": g["L1_ffn_down_bias"],
    }
    nc = bacc.Bacc("TRN2", target_bir_lowering=False, num_devices=1, dynamic_dma_scratch_size=1024)
    arrays, aps = {}, {}
    for name, v in host.items():
        v = np.ascontiguousarray(v)
        arrays["in_" + name] = v
        aps[name] = nc.dram_tensor("in_" + name, v.shape, mybir.dt.from_np(v.dtype), kind="ExternalInput").ap()
    out = nc.dram_tensor("out", (NB, T, D), F32, kind="ExternalOutput").ap()
    build(nc, aps, out)
    r = run_bass_kernel_spmd(nc, [arrays], core_ids=[0])
    return r.results[0]["out"]
```
